# Optimizing a Trainium2 kernel written in Bass

```python
import numpy as np
import jax
import jax.numpy as jnp

def _softmax(x, axis=-1):
    return jax.nn.softmax(x, axis=axis)

def _gelu(x):
    return jax.nn.gelu(x, approximate=True)

def _silu(x):
    return jax.nn.silu(x)

def _sigmoid(x):
    return jax.nn.sigmoid(x)

def _layernorm(x, axis=-1, eps=1e-05):
    m = jnp.mean(x, axis=axis, keepdims=True)
    v = jnp.var(x, axis=axis, keepdims=True)
    return (x - m) / jnp.sqrt(v + eps)

def _scatter_add(tgt, idx, src, axis=0):
    return tgt.at[idx].add(src)

def _segment_sum(src, seg, n):
    return jax.ops.segment_sum(src, seg, n)
kernel_name = 'mk_lm_tower_d1_tok_ids1024_r4_df337a'

def setup_inputs(seed: int=0):
    np.random.seed(seed)
    _w = jnp.asarray

    def _rec_inputs():
        import jax
        import jax.numpy as jnp
        _rk = jax.random.key(seed)
        x = jax.random.randint(jax.random.fold_in(_rk, 1), (8, 512), 0, 7999, jnp.int32)
        return x
    x = _rec_inputs()

    def _L0_tok_setup():
        import jax, jax.numpy as jnp
        import numpy as np
        VOCAB = 8000
        EMBED = 256
        key = jax.random.key(seed)
        k_ids, k_w = jax.random.split(key)
        token_ids = jax.random.randint(k_ids, (4, 512), 0, VOCAB, dtype=jnp.int64 if jax.config.jax_enable_x64 else jnp.int32)
        weight = jax.random.truncated_normal(k_w, -3.0, 3.0, (VOCAB, EMBED), dtype=jnp.float32)
        return {'token_ids': token_ids, 'weight': weight}
    _L0_tok_all = _L0_tok_setup()
    _L0_tok_in = {k: v for k, v in _L0_tok_all.items() if k in ('weight',)}
    del _L0_tok_all

    def _L0_attn_setup():
        import jax, jax.numpy as jnp
        import numpy as np
        INF_APPROX = 1e+30
        ROTARY_BASE = 10000.0
        D_HEAD = 128

        def _rope(x, base=ROTARY_BASE):
            _, length, _, width = x.shape
            half = width // 2
            positions = jnp.arange(length, dtype=x.dtype)
            dims = jnp.arange(half, dtype=x.dtype)
            ang_freqs = jnp.power(base, -dims / half)
            radians = positions[:, None] * ang_freqs[None, :]
            cos = jnp.cos(radians)[None, :, None, :]
            sin = jnp.sin(radians)[None, :, None, :]
            even, odd = jnp.split(x, 2, axis=-1)
            return jnp.concatenate([even * cos - odd * sin, even * sin + odd * cos], axis=-1)
        key = jax.random.key(seed)
        k1, k2, k3, k4, k5 = jax.random.split(key, 5)
        B, T, M, H, D = (2, 1024, 256, 8, 128)
        n_layer = 24
        x = jax.random.normal(k1, (B, T, M), dtype=jnp.float32)
        std_qkv = M ** (-0.5)
        std_o = (M * 2 * n_layer) ** (-0.5)
        w_aq = jnp.zeros((M, H, D), dtype=jnp.float32)
        w_ak = std_qkv * jax.random.normal(k3, (M, H, D), dtype=jnp.float32)
        w_av = std_qkv * jax.random.normal(k4, (M, H, D), dtype=jnp.float32)
        w_ao = std_o * jax.random.normal(k5, (H, D, M), dtype=jnp.float32)
        return {'x': x, 'w_aq': w_aq, 'w_ak': w_ak, 'w_av': w_av, 'w_ao': w_ao}
    _L0_attn_all = _L0_attn_setup()
    _L0_attn_in = {k: v for k, v in _L0_attn_all.items() if k in ('w_aq', 'w_ak', 'w_av', 'w_ao')}
    del _L0_attn_all

    def _L0_ffn_setup():
        import jax, jax.numpy as jnp
        import numpy as np
        from math import ceil
        CAPACITY_FACTOR = 2.0
        MIN_CAPACITY = 4
        key = jax.random.key(seed)
        ks = jax.random.split(key, 4)
        B, S, D, Di, E = (4, 512, 256, 1024, 8)
        x = jax.random.normal(ks[0], (B, S, D), dtype=jnp.float32)
        Wr = jax.random.normal(ks[1], (D, E), dtype=jnp.float32) * D ** (-0.5)
        W1 = jax.random.normal(ks[2], (E, D, Di), dtype=jnp.float32) * D ** (-0.5)
        b1 = jnp.zeros((E, Di), dtype=jnp.float32)
        W2 = jax.random.normal(ks[3], (E, Di, D), dtype=jnp.float32) * Di ** (-0.5)
        b2 = jnp.zeros((E, D), dtype=jnp.float32)
        return {'x': x, 'Wr': Wr, 'W1': W1, 'b1': b1, 'W2': W2, 'b2': b2}
    _L0_ffn_all = _L0_ffn_setup()
    _L0_ffn_in = {k: v for k, v in _L0_ffn_all.items() if k in ('Wr', 'W1', 'b1', 'W2', 'b2')}
    del _L0_ffn_all
    return {'x': x, 'L0_tok_weight': _L0_tok_in['weight'], 'L0_attn_w_aq': _L0_attn_in['w_aq'], 'L0_attn_w_ak': _L0_attn_in['w_ak'], 'L0_attn_w_av': _L0_attn_in['w_av'], 'L0_attn_w_ao': _L0_attn_in['w_ao'], 'L0_ffn_Wr': _L0_ffn_in['Wr'], 'L0_ffn_W1': _L0_ffn_in['W1'], 'L0_ffn_b1': _L0_ffn_in['b1'], 'L0_ffn_W2': _L0_ffn_in['W2'], 'L0_ffn_b2': _L0_ffn_in['b2']}

def reference(x, L0_tok_weight, L0_attn_w_aq, L0_attn_w_ak, L0_attn_w_av, L0_attn_w_ao, L0_ffn_Wr, L0_ffn_W1, L0_ffn_b1, L0_ffn_W2, L0_ffn_b2):
    import jax
    import jax.numpy as jnp

    def _L0_tok_ref(token_ids, weight):
        import jax, jax.numpy as jnp
        import numpy as np
        VOCAB = 8000
        EMBED = 256
        return jnp.take(weight, token_ids, axis=0)

    def _L0_attn_ref(x, w_aq, w_ak, w_av, w_ao):
        import jax, jax.numpy as jnp
        import numpy as np
        INF_APPROX = 1e+30
        ROTARY_BASE = 10000.0
        D_HEAD = 128

        def _rope(x, base=ROTARY_BASE):
            _, length, _, width = x.shape
            half = width // 2
            positions = jnp.arange(length, dtype=x.dtype)
            dims = jnp.arange(half, dtype=x.dtype)
            ang_freqs = jnp.power(base, -dims / half)
            radians = positions[:, None] * ang_freqs[None, :]
            cos = jnp.cos(radians)[None, :, None, :]
            sin = jnp.sin(radians)[None, :, None, :]
            even, odd = jnp.split(x, 2, axis=-1)
            return jnp.concatenate([even * cos - odd * sin, even * sin + odd * cos], axis=-1)
        B, T, M = x.shape
        q = jnp.einsum('btm,mhd->bthd', x, w_aq)
        k = jnp.einsum('btm,mhd->bthd', x, w_ak)
        v = jnp.einsum('btm,mhd->bthd', x, w_av)
        q = _rope(q)
        k = _rope(k)
        s = jnp.einsum('bihd,bjhd->bhij', q, k) / D_HEAD
        i = jnp.arange(T)[:, None]
        j = jnp.arange(T)[None, :]
        mask = (i < j).astype(x.dtype)[None, None, :, :]
        s = s - jnp.asarray(INF_APPROX, x.dtype) * mask
        p = jax.nn.softmax(s, axis=-1)
        o = jnp.einsum('bhij,bjhd->bihd', p, v)
        r = jnp.einsum('bihd,hdm->bim', o, w_ao)
        return r

    def _L0_ffn_ref(x, Wr, W1, b1, W2, b2):
        import jax, jax.numpy as jnp
        import numpy as np
        from math import ceil
        CAPACITY_FACTOR = 2.0
        MIN_CAPACITY = 4
        B, S, D = x.shape
        E = Wr.shape[1]
        N = B * S
        k = max(MIN_CAPACITY, ceil(N * CAPACITY_FACTOR / E))
        xt = x.reshape(N, D)
        scores = jax.nn.softmax(xt @ Wr, axis=-1)
        G, idx = jax.lax.top_k(scores.T, k)
        X_in = xt[idx]
        h = jax.nn.gelu(jnp.einsum('ekd,edh->ekh', X_in, W1) + b1[:, None, :], approximate=False)
        X_e = jnp.einsum('ekh,ehd->ekd', h, W2) + b2[:, None, :]
        contrib = (G[..., None] * X_e).reshape(E * k, D)
        out = jnp.zeros((N, D), dtype=x.dtype).at[idx.reshape(-1)].add(contrib)
        return out.reshape(B, S, D)
    h = _L0_tok_ref(x, L0_tok_weight)
    h = h + _L0_attn_ref(_layernorm(h, axis=-1), L0_attn_w_aq, L0_attn_w_ak, L0_attn_w_av, L0_attn_w_ao)
    h = h + _L0_ffn_ref(_layernorm(h, axis=-1), L0_ffn_Wr, L0_ffn_W1, L0_ffn_b1, L0_ffn_W2, L0_ffn_b2)
    return h

_drawn_inputs = setup_inputs


def setup_inputs(seed=0):
    import zlib

    import numpy as np

    out = dict(_drawn_inputs(seed))
    spreads = {'L0_attn_w_aq': (0.0, 0.675), 'L0_ffn_b1': (0.0, 0.267), 'L0_ffn_b2': (0.0, 0.1)}
    factors = {'L0_attn_w_ak': 5.539}
    for name, (base, spread) in spreads.items():
        noise = np.random.default_rng([zlib.crc32(name.encode()), seed]).standard_normal(out[name].shape)
        drawn = base * np.exp(spread * noise) if base else spread * noise
        out[name] = jnp.asarray(drawn.astype(out[name].dtype))
    for name, factor in factors.items():
        out[name] = (out[name] * factor).astype(out[name].dtype)
    return out
```

```python
import concourse.bass as bass
from concourse import mybir
from concourse.alu_op_type import AluOpType as ALU
from contextlib import ExitStack

F32 = mybir.dt.float32
F32R = mybir.dt.float32r
BF16 = mybir.dt.bfloat16
I32 = mybir.dt.int32
ACT = mybir.ActivationFunctionType
AX = mybir.AxisListType

P = 128
B, T, M = 8, 512, 256
H, D = 8, 128
VOCAB = 8000
N = B * T
TB = T // P
KT = M // P
NB = N // P
E, DI, TOPK = 8, 1024, 1024
EPS = 1e-5

ROWS = [(3, 0, 0, 0), (2, 1, 0, 512), (0, 1, 384, 896), (1, 0, 0, 1024)]
P_COL = {ib: col for ib, _, _, col in ROWS}
ROW_AT = {ib: k for k, (ib, _, _, _) in enumerate(ROWS)}
P_COLS = sum((ib + 1) * P for ib in range(TB))
PT_COL = {0: 0, 1: 512, 2: 896, 3: 1152}
T_FILLS = [([(2, 2), (2, 3), (3, 3)], 896), ([(0, 0), (0, 1), (0, 2), (0, 3)], 0),
           ([(1, 1), (1, 2), (1, 3)], 512)]
V_SLOT = {0: [0, 1], 1: [2], 2: [3], 3: [4], 4: [5], 5: [6], 6: [7], 7: []}


def build_attention(nc, a, ident, h2):
    ctx = ExitStack()
    with ctx:
        def sb(name, shape, dt=F32):
            return ctx.enter_context(nc.sbuf_tensor(name, shape, dt))

        def sem(name):
            return ctx.enter_context(nc.semaphore(name))

        w_qkv = {k: [sb(f"w{k}_{p}", [P, KT, H * D], F32R) for p in ("hi", "lo")] for k in "qkv"}
        w_o = [sb(f"wo_{p}", [P, H, M], F32R) for p in ("hi", "lo")]
        rope_k = sb("rope_k", [P, 2, T])
        rope_q = sb("rope_q", [P, 2, T])
        ident_bf = sb("ident_bf", [P, P], BF16)
        mask_bf = sb("mask_bf", [P, P], BF16)
        mask_f = sb("mask_f", [P, P])
        neg_half = sb("neg_half", [P, TB])
        ids = sb("ids", [P, TB], I32)
        emb = sb("emb", [P, TB, M])
        emb_res = sb("emb_res", [P, TB, M])
        xn = sb("xn", [P, TB, M])
        stats = sb("stats", [P, TB, 6])
        mean_var = sb("mean_var", [P, TB, 2])
        rstd = sb("rstd", [P, TB])
        xT = [sb(f"xT_{p}", [P, KT, T], F32R) for p in ("hi", "lo")]
        q_cos, q_sin = sb("q_cos", [P, T]), sb("q_sin", [P, T])
        k_cos, k_sin = sb("k_cos", [P, T]), sb("k_sin", [P, T])
        qT = [sb(f"qT_{p}", [P, 2, T], F32R) for p in ("hi", "lo")]
        kT = [sb(f"kT_{p}", [P, 2, T], F32R) for p in ("hi", "lo")]
        v = [sb(f"v_{p}", [P, 2 * TB, 4 * D], F32R) for p in ("hi", "lo")]
        prob = sb("prob", [P, 2, P_COLS])
        row_min = sb("row_min", [P, 2, TB])
        row_sum = sb("row_sum", [P, 2, TB])
        row_inv = sb("row_inv", [P, 2, TB])
        pT = [sb(f"pT_{p}", [P, P_COLS], F32R) for p in ("hi", "lo")]
        oT = [sb(f"oT_{p}", [P, T], F32R) for p in ("hi", "lo")]

        bank = [ctx.enter_context(nc.psum_tensor(f"bank{i}", [P, 512], F32)) for i in range(8)]
        proj_ps, s_ps, t_ps, o_ps, r_ps = bank[0:2], bank[2:4], bank[4], bank[5], bank[6:8]

        names = """weights_in tables_in w_hi w_lo consts
            ids_in emb_in res_in stats_done aggr_done var_eps rstd_done xn_ready xt_tr xt_hi xt_lo
            q_proj k_proj v_proj q_rope k_rope q_add k_add q_hi k_hi q_lo k_lo v_hi v_lo
            s_done s_min exp_done inv_done norm_done t_done t_hi t_lo o_done o_hi o_lo
            out_done r_evac apart""".split()
        s = {n: sem(n) for n in names}

        block = ctx.enter_context(nc.Block())

        def after(eng, name, count):
            if isinstance(count, int) and count <= 0:
                return
            eng.wait_ge(s[name], count)

        def alone(eng):
            eng.sem_inc(s["apart"], 1)

        def batches(eng, body):
            body(0, range(8), lambda h: h >= 0)
            with eng.Fori(1, B - 1) as b:
                body(b, range(8), lambda h: True)
            body(B - 1, range(11), lambda h: h < H)

        wsrc = {k: a[f"w{k}"].rearrange("(t p) n -> p t n", p=P) for k in "qkv"}
        wraw = {k: h2[:, 8 * i:8 * i + 8, :].rearrange("p (t g) m -> p t (g m)", t=KT)
                for i, k in enumerate("qkv")}
        wraw_o = h2[:, 24:32, :]

        @block.sync
        def _(sp):
            sp.dma_start(ids[:], a["ids"][0]).then_inc(s["ids_in"], 16)
            sp.dma_start(ident[:], a["ident"][:, :]).then_inc(s["tables_in"], 16)
            sp.dma_start(mask_f[:], a["mask"][:, :]).then_inc(s["tables_in"], 16)
            sp.dma_start(rope_k[:], a["rope"][:, :, :]).then_inc(s["tables_in"], 16)
            for k in "qkv":
                sp.dma_start(wraw[k], wsrc[k]).then_inc(s["weights_in"], 16)
            sp.dma_start(wraw_o, a["wo"].rearrange("h d m -> d h m")).then_inc(s["weights_in"], 16)

            def body(b, slots, ok):
                after(sp, "r_evac", b)
                after(sp, "emb_in", (b + 1) * 16 * TB)
                sp.dma_start(emb_res[:], emb[:]).then_inc(s["res_in"], 16)
                if len(slots) == H:
                    sp.dma_start(ids[:], a["ids"][b + 1]).then_inc(s["ids_in"], 16)
            batches(sp, body)

        @block.gpsimd
        def _(pool):
            nc.gpsimd.memset(neg_half[:], -0.5).then_inc(s["consts"], 1)

            def gather(b):
                after(pool, "ids_in", (b + 1) * 16)
                after(pool, "res_in", b * 16)
                after(pool, "xn_ready", b)
                alone(pool)
                for tb in range(TB):
                    pool.indirect_dma_start(emb[:, tb, :], None, a["emb"][:, :],
                                            bass.IndirectOffsetOnAxis(ids[:, tb:tb + 1], 0))\
                        .then_inc(s["emb_in"], 16)

            def rsqrt(b):
                after(pool, "aggr_done", b + 1)
                alone(pool)
                nc.gpsimd.tensor_scalar(rstd[:], mean_var[:, :, 1], EPS, None, ALU.add)\
                    .then_inc(s["var_eps"], 1)
                after(pool, "var_eps", b + 1)
                nc.gpsimd.tensor_tensor(rstd[:], rstd[:], neg_half[:], ALU.pow)\
                    .then_inc(s["rstd_done"], 1)

            def norm(b, h, ks):
                alone(pool)
                for k in ks:
                    ib, _, _, col = ROWS[k]
                    pr = prob[:, h % 2, col:col + (ib + 1) * P]
                    nc.gpsimd.tensor_scalar(pr, pr, row_inv[:, h % 2, k:k + 1], 1.0,
                                            ALU.mult, ALU.mult).then_inc(s["norm_done"], 1)

            def add(b, h, x):
                n = b * H + h
                cos, sin = (q_cos, q_sin) if x == "q" else (k_cos, k_sin)
                after(pool, f"{x}_rope", n + 1)
                nc.gpsimd.tensor_tensor(cos[:], cos[:], sin[:], ALU.add).then_inc(s[f"{x}_add"], 1)

            def low(b, h, x):
                n = b * H + h
                cos, out = (q_cos, qT) if x == "q" else (k_cos, kT)
                after(pool, f"{x}_hi", n + 1)
                nc.gpsimd.tensor_tensor(out[1][:, h % 2, :], cos[:], out[0][:, h % 2, :].bitcast(F32),
                                        ALU.subtract).then_inc(s[f"{x}_lo"], 1)

            pool.wait_ge(s["consts"], 1)
            gather(0)
            rsqrt(0)

            def body(b, slots, ok):
                for h in slots:
                    n = b * H + h
                    if ok(h - 2):
                        after(pool, "inv_done", 2 * (n - 2) + 2)
                        norm(b, h - 2, [3])
                    if ok(h) and h < H:
                        add(b, h, "q")
                        low(b, h, "q")
                        add(b, h, "k")
                    if ok(h - 1):
                        after(pool, "inv_done", 2 * (n - 1) + 1)
                        norm(b, h - 1, [0, 1, 2])
                    if ok(h) and h < H:
                        low(b, h, "k")
                    if len(slots) == H and h == 4:
                        gather(b + 1)
                    if len(slots) == H and h == 5:
                        rsqrt(b + 1)
            batches(pool, body)

        @block.scalar
        def _(act):
            def hi_of(out, in_, name):
                nc.scalar.activation(out, in_, ACT.Copy).then_inc(s[name], 1)

            act.wait_ge(s["tables_in"], 48)
            nc.scalar.activation(ident_bf[:], ident[:], ACT.Copy).then_inc(s["w_hi"], 1)
            nc.scalar.activation(mask_bf[:], mask_f[:], ACT.Copy).then_inc(s["w_hi"], 1)
            nc.scalar.activation(rope_q[:], rope_k[:], ACT.Copy, scale=-1.0 / D)\
                .then_inc(s["w_hi"], 1)
            act.wait_ge(s["weights_in"], 64)
            for k in "qkv":
                hi_of(w_qkv[k][0][:], wraw[k], "w_hi")
            hi_of(w_o[0][:], wraw_o, "w_hi")

            def xt(b):
                for kt in range(KT):
                    after(act, "xt_tr", KT * b + kt + 1)
                    hi_of(xT[0][:, kt, :], proj_ps[kt][:], "xt_hi")

            def exp(b, h, k):
                n = b * H + h
                ib, bk, pc, col = ROWS[k]
                w = (ib + 1) * P
                after(act, "s_min", TB * n + (1, 3, 3, 4)[k])
                after(act, "t_done", 3 * (n - 2) + 3)
                nc.scalar.activation(prob[:, h % 2, col:col + w], s_ps[bk][:, pc:pc + w], ACT.Exp,
                                     bias=row_min[:, h % 2, k:k + 1], scale=-1.0,
                                     accum_out=row_sum[:, h % 2, k:k + 1]).then_inc(s["exp_done"], 1)

            def t_high(b, h, f):
                n = b * H + h
                pairs, col = T_FILLS[f]
                w = len(pairs) * P
                after(act, "t_done", 3 * n + f + 1)
                after(act, "o_done", n)
                hi_of(pT[0][:, col:col + w], t_ps[:, 0:w], "t_hi")

            def qk_high(b, h, x):
                n = b * H + h
                cos, out = (q_cos, qT) if x == "q" else (k_cos, kT)
                after(act, f"{x}_add", n + 1)
                after(act, "s_done", 3 * (n - 2) + 3)
                hi_of(out[0][:, h % 2, :], cos[:], f"{x}_hi")

            def v_high(b, h, i):
                t = V_SLOT[h][i]
                after(act, "v_proj", 2 * TB * b + t + 1)
                after(act, "o_done", (b - 1) * H + 4 * (t // TB) + 4)
                hi_of(v[0][:, t, :], proj_ps[i][:], "v_hi")

            xt(0)

            def body(b, slots, ok):
                for h in slots:
                    n = b * H + h
                    if ok(h - 3):
                        after(act, "o_done", n - 3 + 1)
                        after(act, "out_done", n - 3)
                        hi_of(oT[0][:], o_ps[:], "o_hi")
                    if ok(h - 2):
                        t_high(b, h - 2, 0)
                    if ok(h - 1):
                        exp(b, h - 1, 0)
                    if ok(h) and h < H:
                        qk_high(b, h, "q")
                    if ok(h - 2):
                        t_high(b, h - 2, 1)
                    if ok(h - 1):
                        exp(b, h - 1, 1)
                        exp(b, h - 1, 2)
                    if ok(h) and h < H:
                        for i in range(len(V_SLOT[h])):
                            v_high(b, h, i)
                    if ok(h - 2):
                        t_high(b, h - 2, 2)
                    if ok(h - 1):
                        exp(b, h - 1, 3)
                    if ok(h) and h < H:
                        qk_high(b, h, "k")
                    if len(slots) == H and h == 7:
                        xt(b + 1)
            batches(act, body)

        @block.vector
        def _(dve):
            def low_of(out, in_, hi, name):
                nc.vector.tensor_tensor(out, in_, hi.bitcast(F32), ALU.subtract)\
                    .then_inc(s[name], 1)

            def stats_of(b):
                after(dve, "emb_in", (b + 1) * 16 * TB)
                for tb in range(TB):
                    nc.vector.bn_stats(stats[:, tb, :], emb[:, tb, :]).then_inc(s["stats_done"], 1)
                after(dve, "stats_done", TB * (b + 1))
                alone(dve)
                for tb in range(TB):
                    last = nc.vector.bn_aggr(mean_var[:, tb, :], stats[:, tb, :])
                last.then_inc(s["aggr_done"], 1)

            def normalise(b):
                after(dve, "rstd_done", b + 1)
                after(dve, "xt_tr", KT * b)
                for tb in range(TB):
                    last = nc.vector.tensor_scalar(xn[:, tb, :], emb[:, tb, :], mean_var[:, tb, 0:1],
                                                   rstd[:, tb:tb + 1], ALU.subtract, ALU.mult)
                last.then_inc(s["xn_ready"], 1)

            def xt(b):
                for kt in range(KT):
                    after(dve, "xt_hi", KT * b + kt + 1)
                    low_of(xT[1][:, kt, :], proj_ps[kt][:], xT[0][:, kt, :], "xt_lo")

            def rope(b, h, x):
                n = b * H + h
                ps, table, cos, sin = ((proj_ps[0], rope_q, q_cos, q_sin) if x == "q" else
                                       (proj_ps[1], rope_k, k_cos, k_sin))
                after(dve, f"{x}_proj", n + 1)
                after(dve, f"{x}_lo", n)
                nc.vector.tensor_tensor(cos[:], ps[:], table[:, 0, :], ALU.mult)
                nc.vector.tensor_tensor(sin[0:64, :], ps[64:128, :], table[0:64, 1, :], ALU.mult)
                nc.vector.tensor_tensor(sin[64:128, :], ps[0:64, :], table[64:128, 1, :], ALU.mult)\
                    .then_inc(s[f"{x}_rope"], 1)

            def t_low(b, h, f):
                n = b * H + h
                pairs, col = T_FILLS[f]
                w = len(pairs) * P
                after(dve, "t_hi", 3 * n + f + 1)
                low_of(pT[1][:, col:col + w], t_ps[:, 0:w], pT[0][:, col:col + w], "t_lo")

            def minimum(b, h, k):
                n = b * H + h
                ib, bk, pc, _ = ROWS[k]
                nc.vector.tensor_reduce(row_min[:, h % 2, k:k + 1], s_ps[bk][:, pc:pc + (ib + 1) * P],
                                        AX.X, ALU.min).then_inc(s["s_min"], 1)

            def inverse(b, h, lo, hi):
                nc.vector.reciprocal(row_inv[:, h % 2, lo:hi], row_sum[:, h % 2, lo:hi])\
                    .then_inc(s["inv_done"], 1)

            def evacuate(b):
                after(dve, "out_done", H * (b + 1))
                after(dve, "res_in", 16 * (b + 1))
                if isinstance(b, int) and b == 0:
                    dve.wait_ge(s["w_lo"], 4)
                for i in range(2):
                    last = nc.vector.tensor_tensor(
                        h2[:, bass.ds(b * TB + 2 * i, 2), :],
                        r_ps[i][:].rearrange("p (t m) -> p t m", m=M),
                        emb_res[:, 2 * i:2 * i + 2, :], ALU.add)
                last.then_inc(s["r_evac"], 1)

            stats_of(0)
            after(dve, "w_hi", 7)
            for k in "qkv":
                low_of(w_qkv[k][1][:], wraw[k], w_qkv[k][0][:], "w_lo")
            low_of(w_o[1][:], wraw_o, w_o[0][:], "w_lo")
            normalise(0)
            xt(0)

            def body(b, slots, ok):
                for h in slots:
                    n = b * H + h
                    if ok(h - 3):
                        after(dve, "o_hi", n - 3 + 1)
                        low_of(oT[1][:], o_ps[:], oT[0][:], "o_lo")
                    if ok(h - 2):
                        after(dve, "exp_done", TB * (n - 2) + 4)
                        inverse(b, h - 2, 3, 4)
                    if ok(h) and h < H:
                        rope(b, h, "q")
                    if ok(h - 2):
                        t_low(b, h - 2, 0)
                    if ok(h - 1):
                        after(dve, "s_done", 3 * (n - 1) + 1)
                        minimum(b, h - 1, 0)
                    if ok(h) and h < H:
                        rope(b, h, "k")
                    if ok(h - 2):
                        t_low(b, h - 2, 1)
                    if ok(h - 1):
                        after(dve, "s_done", 3 * (n - 1) + 2)
                        minimum(b, h - 1, 1)
                        minimum(b, h - 1, 2)
                    if ok(h) and h < H:
                        for i, t in enumerate(V_SLOT[h]):
                            after(dve, "v_hi", 2 * TB * b + t + 1)
                            low_of(v[1][:, t, :], proj_ps[i][:], v[0][:, t, :], "v_lo")
                    if ok(h - 2):
                        t_low(b, h - 2, 2)
                    if ok(h - 1):
                        after(dve, "s_done", 3 * (n - 1) + 3)
                        minimum(b, h - 1, 3)
                        after(dve, "exp_done", TB * (n - 1) + 3)
                        inverse(b, h - 1, 0, 3)
                    if h == 2 and ok(h - 3):
                        evacuate(b - 1)
                    if h == 10:
                        evacuate(b)
                    if len(slots) == H and h == 5:
                        stats_of(b + 1)
                    if len(slots) == H and h == 6:
                        normalise(b + 1)
                    if len(slots) == H and h == 7:
                        xt(b + 1)
            batches(dve, body)

        @block.tensor
        def _(pe):
            PARTS = [(0, 0), (0, 1), (1, 0)]

            def products(out, pairs, start=True, stop=True):
                todo = [(l[i], r[j]) for l, r in pairs for i, j in PARTS]
                for c, (l, r) in enumerate(todo):
                    last = nc.tensor.matmul(out, l, r, start=start and c == 0,
                                            stop=stop and c == len(todo) - 1)
                return last

            def xt(b):
                after(pe, "xn_ready", b + 1)
                for kt in range(KT):
                    after(pe, "k_rope" if kt else "q_rope", b * H)
                    for tb in range(TB):
                        last = nc.tensor.transpose(proj_ps[kt][:, tb * P:(tb + 1) * P],
                                                   xn[:, tb, kt * P:(kt + 1) * P], ident[:])
                    last.then_inc(s["xt_tr"], 1)

            def project(b, h, x):
                n = b * H + h
                ps = proj_ps[0 if x == "q" else 1]
                if h == 0:
                    after(pe, "xt_lo", KT * (b + 1))
                elif x == "q":
                    after(pe, "v_lo", 2 * TB * b + V_SLOT[h - 1][-1] + 1)
                elif h == 1:
                    after(pe, "v_lo", 2 * TB * b + 2)
                else:
                    after(pe, "k_rope", n)
                products(ps[:], [([w[:, kt, h * D:(h + 1) * D] for w in w_qkv[x]],
                                  [t[:, kt, :] for t in xT]) for kt in range(KT)])\
                    .then_inc(s[f"{x}_proj"], 1)

            def values(b, h, i):
                n = b * H + h
                g, jb = divmod(V_SLOT[h][i], TB)
                after(pe, "k_rope" if i else "q_rope", n + 1)
                products(proj_ps[i][:], [([t[:, kt, jb * P:(jb + 1) * P] for t in xT],
                                          [w[:, kt, g * 512:(g + 1) * 512] for w in w_qkv["v"]])
                                         for kt in range(KT)]).then_inc(s["v_proj"], 1)

            def scores(b, h, ks):
                n = b * H + h
                for k in ks:
                    ib, bk, pc, _ = ROWS[k]
                    w = (ib + 1) * P
                    products(s_ps[bk][:, pc:pc + w],
                             [([q[:, h % 2, ib * P:(ib + 1) * P] for q in qT],
                               [x[:, h % 2, 0:w] for x in kT])], stop=False)
                    last = nc.tensor.matmul(s_ps[bk][:, pc + ib * P:pc + w], ident_bf[:], mask_bf[:],
                                            start=False, stop=True)
                last.then_inc(s["s_done"], 1)

            def turn(b, h, f):
                n = b * H + h
                after(pe, "t_lo", 3 * n + f)
                for c, (jb, ib) in enumerate(T_FILLS[f][0]):
                    col = P_COL[ib] + jb * P
                    last = nc.tensor.transpose(t_ps[:, c * P:(c + 1) * P],
                                               prob[:, h % 2, col:col + P], ident[:])
                last.then_inc(s["t_done"], 1)

            def weigh(b, h):
                n = b * H + h
                g = (h % H) // 4
                after(pe, "t_lo", 3 * n + 3)
                after(pe, "v_lo", 2 * TB * b + TB * (g + 1) if 0 <= h < H
                      else 2 * TB * (b - 1) + TB * (g + 1))
                after(pe, "o_lo", n)
                order = [0, 2, 3, 1]
                for jb in order:
                    w = T - jb * P
                    c = (h % 4) * D
                    last = products(o_ps[:, jb * P:T],
                                    [([x[:, g * TB + jb, c:c + D] for x in v],
                                      [x[:, PT_COL[jb]:PT_COL[jb] + w] for x in pT])],
                                    start=jb == 0, stop=jb == order[-1])
                last.then_inc(s["o_done"], 1)

            def output(b, h, half):
                n = b * H + h
                hh = h % H
                after(pe, "o_lo", n + 1)
                if hh == 0:
                    after(pe, "r_evac", b if h >= 0 else b - 1)
                for ib in (2 * half, 2 * half + 1):
                    last = products(r_ps[half][:, (ib % 2) * M:(ib % 2 + 1) * M],
                                    [([x[:, ib * P:(ib + 1) * P] for x in oT],
                                      [w[:, hh, :] for w in w_o])],
                                    start=hh == 0 and ib % 2 == 0,
                                    stop=hh == H - 1 and ib % 2 == 1)
                if half:
                    last.then_inc(s["out_done"], 1)

            pe.wait_ge(s["w_lo"], 4)
            xt(0)

            def body(b, slots, ok):
                for h in slots:
                    n = b * H + h
                    if ok(h - 3):
                        weigh(b, h - 3)
                    if ok(h) and h < H:
                        project(b, h, "q")
                    if ok(h - 2):
                        after(pe, "norm_done", TB * (n - 2) + 2)
                        turn(b, h - 2, 0)
                    if ok(h - 1):
                        after(pe, "q_lo", n)
                        after(pe, "k_lo", n)
                        after(pe, "exp_done", TB * (n - 1))
                        scores(b, h - 1, [0])
                    if ok(h - 3):
                        output(b, h - 3, 0)
                    if ok(h) and h < H:
                        project(b, h, "k")
                    if ok(h - 2):
                        after(pe, "norm_done", TB * (n - 2) + 4)
                        turn(b, h - 2, 1)
                    if ok(h - 1):
                        after(pe, "exp_done", TB * (n - 2) + 3)
                        scores(b, h - 1, [1, 2])
                    if ok(h) and h < H:
                        for i in range(len(V_SLOT[h])):
                            values(b, h, i)
                    if ok(h - 2):
                        turn(b, h - 2, 2)
                    if ok(h - 1):
                        after(pe, "exp_done", TB * (n - 1) + 1)
                        scores(b, h - 1, [3])
                    if ok(h - 3):
                        output(b, h - 3, 1)
                    if len(slots) == H and h == 7:
                        xt(b + 1)
            batches(pe, body)
LIST_A = 32
CH = TOPK // P
HALF = 512
DT = DI // P
ROW = M + E


def build_router(nc, a, ident, h2, score):
    ctx = ExitStack()
    with ctx:
        def sb(name, shape, dt=F32):
            return ctx.enter_context(nc.sbuf_tensor(name, shape, dt))

        rows = sb("rows", [P, NB, ROW])
        wr = sb("wr", [P, KT, E])
        stats = sb("r_stats", [P, NB, 6])
        mean_var = sb("r_mean_var", [P, NB, 2])
        rstd = sb("r_rstd", [P, NB])
        neg_half = sb("r_neg_half", [P, NB])
        xT = sb("r_xT", [P, 4, KT, P])
        top = sb("r_top", [P, NB])
        total = sb("r_total", [P, NB])
        logit = sb("r_logit", [P, NB, E])
        x_ps = [ctx.enter_context(nc.psum_tensor(f"rx{i}", [P, 512], F32)) for i in range(4)]
        l_ps = ctx.enter_context(nc.psum_tensor("r_logits", [P, NB, E], F32))
        names = """r_in h2_out rows_out r_const r_stats_done r_aggr r_eps r_rstd_done r_norm
            r_tr r_copy r_logits_done r_step r_exp r_score""".split()
        s = {n: ctx.enter_context(nc.semaphore(n)) for n in names}
        block = ctx.enter_context(nc.Block())

        @block.sync
        def _(sp):
            sp.dma_start(wr[:], a["wr"].rearrange("(t p) e -> p t e", p=P)).then_inc(s["r_in"], 16)
            sp.dma_start(a["out"].rearrange("(b p) m -> p b m", p=P), h2[:]).then_inc(s["h2_out"], 16)
            sp.wait_ge(s["r_score"], 2)
            sp.dma_start(a["rows"].rearrange("(b p) m -> p b m", p=P), rows[:])\
                .then_inc(s["rows_out"], 16)
            sp.wait_ge(s["h2_out"], 16)
            sp.wait_ge(s["rows_out"], 16)

        @block.gpsimd
        def _(pool):
            nc.gpsimd.memset(neg_half[:], -0.5).then_inc(s["r_const"], 1)
            pool.wait_ge(s["r_const"], 1)
            pool.wait_ge(s["r_aggr"], NB)
            nc.gpsimd.tensor_scalar(rstd[:], mean_var[:, :, 1], EPS, None, ALU.add)\
                .then_inc(s["r_eps"], 1)
            pool.wait_ge(s["r_eps"], 1)
            nc.gpsimd.tensor_tensor(rstd[:], rstd[:], neg_half[:], ALU.pow)\
                .then_inc(s["r_rstd_done"], 1)

        @block.vector
        def _(dve):
            step = [0]

            def chained(ins):
                step[0] += 1
                ins.then_inc(s["r_step"], 1)
                dve.wait_ge(s["r_step"], step[0])

            for t in range(NB):
                nc.vector.bn_stats(stats[:, t, :], h2[:, t, :]).then_inc(s["r_stats_done"], 1)
            for t in range(NB):
                dve.wait_ge(s["r_stats_done"], t + 1)
                nc.vector.bn_aggr(mean_var[:, t, :], stats[:, t, :]).then_inc(s["r_aggr"], 1)
            dve.wait_ge(s["r_rstd_done"], 1)
            for t in range(NB):
                nc.vector.tensor_scalar(rows[:, t, 0:M], h2[:, t, :], mean_var[:, t, 0:1],
                                        rstd[:, t:t + 1], ALU.subtract, ALU.mult)\
                    .then_inc(s["r_norm"], 1)
            dve.wait_ge(s["r_logits_done"], NB)
            chained(nc.vector.tensor_reduce(top[:], l_ps[:], AX.X, ALU.max))
            nc.vector.tensor_tensor(logit[:], l_ps[:], top[:].unsqueeze(2).to_broadcast([P, NB, E]),
                                    ALU.subtract).then_inc(s["r_exp"], 1)
            dve.wait_ge(s["r_exp"], 2)
            chained(nc.vector.tensor_reduce(total[:], logit[:], AX.X, ALU.add))
            chained(nc.vector.reciprocal(total[:], total[:]))
            nc.vector.tensor_tensor(rows[:, :, M:ROW], logit[:],
                                    total[:].unsqueeze(2).to_broadcast([P, NB, E]), ALU.mult)\
                .then_inc(s["r_score"], 1)
            nc.vector.tensor_tensor(score[:].rearrange("p e b -> p b e"), logit[:],
                                    total[:].unsqueeze(2).to_broadcast([P, NB, E]), ALU.mult)\
                .then_inc(s["r_score"], 1)

        @block.scalar
        def _(act):
            for t in range(NB):
                act.wait_ge(s["r_tr"], t + 1)
                if t >= 4:
                    act.wait_ge(s["r_logits_done"], t - 3)
                nc.scalar.activation(xT[:, t % 4, :, :].rearrange("p k n -> p (k n)"),
                                     x_ps[t % 4][:, 0:KT * P], ACT.Copy).then_inc(s["r_copy"], 1)
            act.wait_ge(s["r_exp"], 1)
            nc.scalar.activation(logit[:], logit[:], ACT.Exp).then_inc(s["r_exp"], 1)

        @block.tensor
        def _(pe):
            pe.wait_ge(s["r_in"], 16)
            for t in range(NB + 2):
                if t < NB:
                    pe.wait_ge(s["r_norm"], t + 1)
                    if t >= 4:
                        pe.wait_ge(s["r_copy"], t - 3)
                    for kt in range(KT):
                        last = nc.tensor.transpose(x_ps[t % 4][:, kt * P:(kt + 1) * P],
                                                   rows[:, t, kt * P:(kt + 1) * P], ident[:])
                    last.then_inc(s["r_tr"], 1)
                if t >= 2:
                    u = t - 2
                    pe.wait_ge(s["r_copy"], u + 1)
                    for kt in range(KT):
                        last = nc.tensor.matmul(l_ps[:, u, :], xT[:, u % 4, kt, :], wr[:, kt, :],
                                                start=kt == 0, stop=kt == KT - 1)
                    last.then_inc(s["r_logits_done"], 1)


def build_experts(nc, a, ident, score):
    ctx = ExitStack()
    with ctx:
        def sb(name, shape, dt=F32):
            return ctx.enter_context(nc.sbuf_tensor(name, shape, dt))

        def ps(name, shape=(P, 512)):
            return ctx.enter_context(nc.psum_tensor(name, list(shape), F32))

        tri_f, tri = sb("tri_f", [P, P]), sb("tri", [P, P], BF16)
        ones = sb("ones", [P, P], BF16)
        least = sb("least", [P, E], I32)
        bit = sb("bit", [P, E], I32)
        cand = sb("cand", [P, E], I32)
        enough = sb("enough", [P, E], I32)
        above = sb("above", [P, E, NB], BF16)
        equal = sb("equal", [P, E, NB], BF16)
        chosen = sb("chosen", [P, E, NB], BF16)
        count_bf = sb("count_bf", [P, E], BF16)
        need = sb("need", [P, E])
        restart = sb("restart", [P, E, NB])
        rank = sb("rank", [P, E, NB])
        place = sb("place", [P, E, NB], I32)
        place_a, place_b = sb("place_a", [P, E, NB], I32), sb("place_b", [P, E, NB], I32)
        at_a, at_b = sb("at_a", [P, E, NB], BF16), sb("at_b", [P, E, NB], BF16)
        iota_i = sb("iota_i", [P, LIST_A], I32)
        iota32 = sb("iota32", [P, LIST_A], BF16)
        blk_i = sb("blk_i", [P, NB], I32)
        blk_no = sb("blk_no", [P, NB], BF16)
        tok_i = sb("tok_i", [P, 1], I32)
        tok_no = sb("tok_no", [P, 1])
        hot_a = sb("hot_a", [P, NB, LIST_A], BF16)
        hot_b = sb("hot_b", [P, NB, 3, LIST_A], BF16)
        list_tok = sb("list_tok", [LIST_A, LIST_A])
        list_f = sb("list_f", [LIST_A, LIST_A])
        tokens = [sb(f"tokens{i}", [P, CH], I32) for i in range(2)]
        raw1, raw2 = sb("raw1", [P, KT, DI]), sb("raw2", [P, DT, M])
        w1 = [[sb(f"w1_{i}{p}", [P, KT, DI], F32R) for p in ("hi", "lo")] for i in range(2)]
        w2 = [[sb(f"w2_{i}{p}", [P, DT, M], F32R) for p in ("hi", "lo")] for i in range(2)]
        b1_rows = sb("b1_rows", [E * DT, P])
        b1 = sb("b1", [P, E * DT])
        b1_e = [sb(f"b1_e{i}", [P, DT]) for i in range(2)]
        b2 = sb("b2", [P, E, M])
        got = [sb(f"got{i}", [P, CH, ROW]) for i in range(2)]
        gate = [sb(f"gate{i}", [P, CH]) for i in range(2)]
        xT = [[sb(f"e_xT{i}{p}", [P, KT, TOPK], F32R) for p in ("hi", "lo")] for i in range(2)]
        hid = sb("hid", [P, 2, HALF])
        hT = [sb(f"hT_{p}", [P, 4, HALF], F32R) for p in ("hi", "lo")]
        y = [sb(f"y{i}", [P, TB, M]) for i in range(2)]

        up_ps = [ps("up0"), ps("up1")]
        y_ps = [[ps("y00"), ps("y01")], [ps("y10"), ps("y11")]]
        x_ps, l_ps = ps("x_ps"), ps("l_ps")

        names = """c_in c_const c_const2 c_const3 c_step counted totalled marked ranked b1_tr b1_ready
            raw_in w_hi2 w_lo2 up_done down_done h_hi h_lo e_xt_tr e_xt_hi e_xt_lo hot_ready listed
            tok_ready rows_in gate_ready y_b2 y_gated added0 added1 l_chain e_apart""".split()
        s = {n: ctx.enter_context(nc.semaphore(n)) for n in names}
        block = ctx.enter_context(nc.Block())

        def after(eng, name, count):
            if isinstance(count, int) and count <= 0:
                return
            eng.wait_ge(s[name], count)

        def alone(eng):
            eng.sem_inc(s["e_apart"], 1)

        STEPS = 2 * DT
        RING = 4
        LAG = 2

        def experts(eng, body):
            for i in range(2):
                body(i, i, True)
            with eng.Fori(1, E // 2 - 1) as j:
                for i in range(2):
                    body(j * 2 + i, i, True)
            for i in range(2):
                body(E - 2 + i, i, i == 0)

        def wide(x):
            return x.unsqueeze(2).to_broadcast([P, E, NB])

        @block.sync
        def _(sp):
            sp.dma_start(tri_f[:], a["tri"][:, :]).then_inc(s["c_in"], 16)
            sp.dma_start(b1_rows[:], a["b1"].rearrange("e (t p) -> (e t) p", p=P))\
                .then_inc(s["c_in"], 16)
            sp.dma_start(b2[:], a["b2"].rearrange("(o e) m -> o e m", o=1).to_broadcast([P, E, M]))\
                .then_inc(s["c_in"], 16)

            def load(e):
                after(sp, "w_lo2", 2 * e)
                sp.dma_start(raw1[:], a["w1"][e].rearrange("(t p) n -> p t n", p=P))\
                    .then_inc(s["raw_in"], 16)
                sp.dma_start(raw2[:], a["w2"][e].rearrange("(t p) m -> p t m", p=P))\
                    .then_inc(s["raw_in"], 16)
            load(0)
            experts(sp, lambda e, i, more: load(e + 1) if more else None)
            for half in range(2):
                sp.wait_ge(s[f"added{half}"], 16 * TB * E)

        @block.gpsimd
        def _(pool):
            nc.gpsimd.iota(iota_i[:], [[1, LIST_A]], base=0, channel_multiplier=0)\
                .then_inc(s["c_const"], 1)
            nc.gpsimd.iota(blk_i[:], [[1, NB]], base=0, channel_multiplier=0)\
                .then_inc(s["c_const"], 1)
            nc.gpsimd.iota(tok_i[:], [[1, 1]], base=0, channel_multiplier=1)\
                .then_inc(s["c_const"], 1)
            nc.gpsimd.memset(ones[:], 1.0).then_inc(s["c_const"], 1)
            nc.gpsimd.memset(bit[:], 1 << 29).then_inc(s["c_const"], 1)
            nc.gpsimd.memset(least[:], 0).then_inc(s["c_const"], 1)
            nc.gpsimd.memset(restart[:], 1.0).then_inc(s["c_const2"], 1)
            pool.wait_ge(s["c_const2"], 1)
            nc.gpsimd.memset(restart[:, :, 0:1], 0.0).then_inc(s["c_const"], 1)

            def gather(e, i):
                after(pool, "tok_ready", e + 1)
                after(pool, "e_xt_tr", 4 * (e - 1))
                after(pool, "gate_ready", e - 1)
                alone(pool)
                for c in range(CH):
                    pool.indirect_dma_start(got[i][:, c, :], None, a["rows"][:, :],
                                            bass.IndirectOffsetOnAxis(tokens[i][:, c:c + 1], 0))\
                        .then_inc(s["rows_in"], 16)

            def add(e, i, half):
                u = 2 * e + half
                after(pool, "gate_ready", e + 1)
                after(pool, "y_b2", 2 * u + 2)
                alone(pool)
                for c in range(TB):
                    nc.gpsimd.tensor_scalar(y[half][:, c, :], y[half][:, c, :],
                                            gate[i][:, TB * half + c:TB * half + c + 1], 1.0,
                                            ALU.mult, ALU.mult).then_inc(s["y_gated"], 1)
                if half == 0:
                    for k in range(2):
                        after(pool, f"added{k}", 16 * TB * e)
                for c in range(TB):
                    after(pool, "y_gated", TB * u + c + 1)
                    alone(pool)
                    pool.indirect_dma_start(a["out"][:, :],
                                            bass.IndirectOffsetOnAxis(
                                                tokens[i][:, TB * half + c:TB * half + c + 1], 0),
                                            y[half][:, c, :], None, compute_op=ALU.add)\
                        .then_inc(s[f"added{half}"], 16)

            gather(0, 0)

            def body(e, i, more):
                if not (isinstance(e, int) and e == 0):
                    add(e - 1, 1 - i, 1)
                if more:
                    gather(e + 1, 1 - i)
                add(e, i, 0)
            experts(pool, body)
            add(E - 1, 1, 1)

        @block.vector
        def _(dve):
            step = [0]

            def chained(ins):
                step[0] += 1
                ins.then_inc(s["c_step"], 1)
                dve.wait_ge(s["c_step"], step[0])

            dve.wait_ge(s["c_in"], 48)
            dve.wait_ge(s["c_const"], 7)
            nc.vector.tensor_copy(tri[:], tri_f[:])
            nc.vector.tensor_copy(iota32[:], iota_i[:]).then_inc(s["l_chain"], 1)
            nc.vector.tensor_copy(blk_no[:], blk_i[:])
            chained(nc.vector.tensor_copy(tok_no[:], tok_i[:]))
            dve.wait_ge(s["b1_tr"], 1)
            nc.vector.tensor_copy(b1[:], l_ps[:, 0:E * DT]).then_inc(s["b1_ready"], 1)

            def count_marks():
                with nc.allow_low_precision(reason="counts up to 32 are exact in bfloat16"):
                    nc.vector.tensor_reduce(count_bf[:], above[:], AX.X, ALU.add)\
                        .then_inc(s["counted"], 1)

            ITERATIONS = 30
            with dve.Fori(0, ITERATIONS) as r:
                dve.wait_ge(s["l_chain"], r * 5 + 1)
                nc.vector.tensor_tensor(cand[:], least[:], bit[:], ALU.bitwise_or)\
                    .then_inc(s["l_chain"], 1)
                dve.wait_ge(s["l_chain"], r * 5 + 2)
                nc.vector.tensor_tensor(above[:], score[:], wide(cand[:].bitcast(F32)), ALU.is_ge)\
                    .then_inc(s["l_chain"], 1)
                dve.wait_ge(s["l_chain"], r * 5 + 3)
                count_marks()
                nc.vector.tensor_scalar(bit[:], bit[:], 1, None, ALU.logical_shift_right)\
                    .then_inc(s["l_chain"], 1)
                dve.wait_ge(s["totalled"], r + 1)
                nc.vector.tensor_scalar(enough[:], l_ps[:, 0:E], float(TOPK), None, ALU.is_ge)\
                    .then_inc(s["l_chain"], 1)
                dve.wait_ge(s["l_chain"], r * 5 + 5)
                alone(dve)
                nc.vector.copy_predicated(least[:], enough[:], cand[:]).then_inc(s["l_chain"], 1)
            dve.wait_ge(s["l_chain"], ITERATIONS * 5 + 1)

            def ranks(k):
                dve.wait_ge(s["ranked"], k)
                before, per_block = l_ps[:, 0:E * NB], l_ps[:, E * NB:2 * E * NB]
                flat = rank[:].rearrange("p e b -> p (e b)")
                chained(nc.vector.tensor_tensor_scan(
                    flat, restart[:].rearrange("p e b -> p (e b)"), per_block, 0.0,
                    ALU.mult, ALU.add))
                chained(nc.vector.tensor_tensor(flat, per_block, flat, ALU.subtract))
                chained(nc.vector.tensor_tensor(flat, before, flat, ALU.subtract))

            edge = wide(least[:].bitcast(F32))
            chained(nc.vector.tensor_tensor(above[:], score[:], edge, ALU.is_gt))
            count_marks()
            dve.wait_ge(s["totalled"], ITERATIONS + 1)
            chained(nc.vector.tensor_scalar(need[:], l_ps[:, 0:E], -1.0, float(TOPK),
                                            ALU.mult, ALU.add))
            nc.vector.tensor_tensor(equal[:], score[:], edge, ALU.is_equal)\
                .then_inc(s["marked"], 1)
            ranks(1)
            chained(nc.vector.tensor_tensor(rank[:], rank[:], wide(need[:]), ALU.is_lt))
            chained(nc.vector.tensor_tensor(chosen[:], rank[:], equal[:], ALU.mult))
            nc.vector.tensor_tensor(chosen[:], chosen[:], above[:], ALU.add)\
                .then_inc(s["marked"], 1)
            ranks(2)
            chained(nc.vector.tensor_scalar(score[:], chosen[:], -4.0 * TOPK, 4.0 * TOPK,
                                            ALU.mult, ALU.add))
            chained(nc.vector.tensor_tensor(place[:], rank[:], score[:], ALU.add))
            chained(nc.vector.tensor_scalar(place_a[:], place[:], 5, None, ALU.logical_shift_right))
            chained(nc.vector.tensor_scalar(place_b[:], place[:], LIST_A - 1, None, ALU.bitwise_and))
            nc.vector.tensor_copy(at_a[:], place_a[:])
            chained(nc.vector.tensor_copy(at_b[:], place_b[:]))

            chain0 = ITERATIONS * 5 + 1

            def one_hots(e):
                after(dve, "listed", e)
                wide_iota = iota32[:].unsqueeze(1).to_broadcast([P, NB, LIST_A])

                def spread(x):
                    return x[:, bass.ds(e, 1), :].rearrange("p o b -> p (o b)").unsqueeze(2)\
                        .to_broadcast([P, NB, LIST_A])
                nc.vector.tensor_tensor(hot_a[:], spread(at_a), wide_iota, ALU.is_equal)
                nc.vector.tensor_tensor(hot_b[:, :, 0, :], spread(at_b), wide_iota, ALU.is_equal)\
                    .then_inc(s["l_chain"], 1)
                dve.wait_ge(s["l_chain"], e * 3 + (chain0 + 1))
                nc.vector.tensor_scalar(hot_b[:, :, 1, :], hot_b[:, :, 0, :], tok_no[:, 0:1], None,
                                        ALU.mult)
                nc.vector.tensor_tensor(hot_b[:, :, 2, :], hot_b[:, :, 0, :],
                                        blk_no[:].unsqueeze(2).to_broadcast([P, NB, LIST_A]),
                                        ALU.mult).then_inc(s["hot_ready"], 1)

            def write_list(e, i):
                after(dve, "listed", e + 1)
                for k in range(2):
                    after(dve, f"added{k}", 16 * TB * (e - 1))
                nc.vector.tensor_copy(list_tok[:], l_ps[0:LIST_A, 0:LIST_A]).then_inc(s["l_chain"], 1)
                dve.wait_ge(s["l_chain"], e * 3 + (chain0 + 2))
                nc.vector.scalar_tensor_tensor(list_f[:], l_ps[0:LIST_A, LIST_A:2 * LIST_A], float(P),
                                               list_tok[:], ALU.mult, ALU.add)\
                    .then_inc(s["l_chain"], 1)
                dve.wait_ge(s["l_chain"], e * 3 + (chain0 + 3))
                for q in range(P // LIST_A):
                    last = nc.vector.tensor_copy(
                        tokens[i][q * LIST_A:(q + 1) * LIST_A, :],
                        list_f[:].rearrange("a (c q) -> a q c", q=P // LIST_A)[:, q, :])
                last.then_inc(s["tok_ready"], 1)

            def low(out, in_, hi, name):
                nc.vector.tensor_tensor(out, in_, hi.bitcast(F32), ALU.subtract)\
                    .then_inc(s[name], 1)

            def split_weights(e, i, which):
                raw, w = ((raw1, w1), (raw2, w2))[which]
                after(dve, "w_hi2", 2 * e + which + 1)
                low(w[i][1][:], raw[:], w[i][0][:], "w_lo2")

            def first_bias(e, i):
                after(dve, "b1_ready", e + 1)
                after(dve, "h_hi", STEPS * (e - 1))
                nc.vector.tensor_scalar(b1_e[i][:], b1[:, bass.ds(e * DT, DT)], 1.0, None, ALU.mult)\
                    .then_inc(s["b1_ready"], 1)

            def gates(e, i):
                after(dve, "rows_in", 16 * CH * (e + 1))
                after(dve, "y_gated", CH * (e - 1))
                nc.vector.tensor_scalar(gate[i][:],
                                        got[i][:, :, bass.ds(e + M, 1)].rearrange("p c o -> p (c o)"),
                                        1.0, None, ALU.mult).then_inc(s["gate_ready"], 1)

            def xt_low(e, i, f):
                kt, g = divmod(f, 2)
                after(dve, "e_xt_hi", 4 * e + f + 1)
                cols = slice(g * HALF, (g + 1) * HALF)
                low(xT[i][1][:, kt, cols], x_ps[:], xT[i][0][:, kt, cols], "e_xt_lo")

            def results(e, half):
                u = 2 * e + half
                after(dve, "down_done", DT * (u + 1))
                after(dve, f"added{half}", 16 * TB * e)
                for k in range(2):
                    nc.vector.tensor_tensor(
                        y[half][:, 2 * k:2 * k + 2, :],
                        y_ps[half][k][:].rearrange("p (c m) -> p c m", m=M),
                        b2[:, bass.ds(e, 1), :].to_broadcast([P, 2, M]), ALU.add)\
                        .then_inc(s["y_b2"], 1)

            one_hots(0)
            write_list(0, 0)
            first_bias(0, 0)
            split_weights(0, 0, 0)
            split_weights(0, 0, 1)
            gates(0, 0)
            for f in range(4):
                xt_low(0, 0, f)

            def body(e, i, more):
                for t in range(STEPS):
                    k = e * STEPS + t
                    after(dve, "h_hi", k + 1)
                    low(hT[1][:, t % RING, :], hid[:, t % 2, :],
                        hT[0][:, t % RING, :], "h_lo")
                    if t == LAG and not (isinstance(e, int) and e == 0):
                        results(e - 1, 1)
                    if t == DT + LAG:
                        results(e, 0)
                    if more:
                        if t == 0:
                            one_hots(e + 1)
                        if t == 5:
                            write_list(e + 1, 1 - i)
                            first_bias(e + 1, 1 - i)
                        if t in (6, 8):
                            split_weights(e + 1, 1 - i, (t - 6) // 2)
                        if t == 12:
                            gates(e + 1, 1 - i)
                        if 12 <= t < 16:
                            xt_low(e + 1, 1 - i, t - 12)
            experts(dve, body)
            results(E - 1, 1)

        @block.scalar
        def _(act):
            def hi_of(out, in_, name):
                nc.scalar.activation(out, in_, ACT.Copy).then_inc(s[name], 1)

            def split_weights(e, i, which):
                raw, w = ((raw1, w1), (raw2, w2))[which]
                after(act, "raw_in", 32 * (e + 1))
                after(act, "down_done", STEPS * (e - 1))
                hi_of(w[i][0][:], raw[:], "w_hi2")

            def xt_high(e, i, f):
                kt, g = divmod(f, 2)
                after(act, "e_xt_tr", 4 * e + f + 1)
                after(act, "up_done", STEPS * (e - 1))
                hi_of(xT[i][0][:, kt, g * HALF:(g + 1) * HALF], x_ps[:], "e_xt_hi")

            split_weights(0, 0, 0)
            split_weights(0, 0, 1)
            for f in range(4):
                xt_high(0, 0, f)

            def body(e, i, more):
                after(act, "b1_ready", e + 2)
                for t in range(STEPS):
                    k = e * STEPS + t
                    bias = b1_e[i][:, t % DT:t % DT + 1]
                    after(act, "up_done", k + 1)
                    after(act, "h_lo", k - 1)
                    nc.scalar.activation(hid[:, t % 2, :], up_ps[t % 2][:], ACT.Gelu, bias=bias)
                    after(act, "down_done", k - (RING - 1))
                    nc.scalar.activation(hT[0][:, t % RING, :], up_ps[t % 2][:], ACT.Gelu,
                                         bias=bias).then_inc(s["h_hi"], 1)
                    if more:
                        if t in (5, 7):
                            split_weights(e + 1, 1 - i, (t - 5) // 2)
                        if 12 <= t < 16:
                            xt_high(e + 1, 1 - i, t - 12)
            experts(act, body)

        @block.tensor
        def _(pe):
            PARTS = [(0, 0), (0, 1), (1, 0)]

            pe.wait_ge(s["c_in"], 48)
            nc.tensor.transpose(l_ps[:, 0:E * DT], b1_rows[:], ident[0:E * DT, 0:E * DT])\
                .then_inc(s["b1_tr"], 1)
            pe.wait_ge(s["b1_ready"], 1)
            with pe.Fori(0, 30) as r:
                pe.wait_ge(s["counted"], r + 1)
                nc.tensor.matmul(l_ps[:, 0:E], ones[:], count_bf[:], start=True, stop=True)\
                    .then_inc(s["totalled"], 1)
            pe.wait_ge(s["counted"], 31)
            nc.tensor.matmul(l_ps[:, 0:E], ones[:], count_bf[:], start=True, stop=True)\
                .then_inc(s["totalled"], 1)
            for k, mark in enumerate((equal, chosen)):
                pe.wait_ge(s["marked"], k + 1)
                flat = mark[:].rearrange("p e b -> p (e b)")
                nc.tensor.matmul(l_ps[:, 0:E * NB], tri[:], flat, start=True, stop=True)
                nc.tensor.matmul(l_ps[:, E * NB:2 * E * NB], ones[:], flat, start=True, stop=True)\
                    .then_inc(s["ranked"], 1)

            def write_list(e):
                after(pe, "hot_ready", e + 1)
                after(pe, "tok_ready", e)
                for t in range(NB):
                    last = nc.tensor.matmul(l_ps[0:LIST_A, 0:2 * LIST_A], hot_a[:, t, :],
                                            hot_b[:, t, 1:3, :].rearrange("p k b -> p (k b)"),
                                            start=t == 0, stop=t == NB - 1)
                last.then_inc(s["listed"], 1)

            def turn(e, i, f):
                kt, g = divmod(f, 2)
                after(pe, "rows_in", 16 * CH * (e + 1))
                after(pe, "e_xt_lo", 4 * e + f)
                for c in range(TB):
                    last = nc.tensor.transpose(x_ps[:, c * P:(c + 1) * P],
                                               got[i][:, TB * g + c, kt * P:(kt + 1) * P], ident[:])
                last.then_inc(s["e_xt_tr"], 1)

            def up(e, i, t):
                k = e * STEPS + t
                half, dt = divmod(t, DT)
                after(pe, "h_hi", k - 1)
                todo = [(w1[i][x][:, kt, dt * P:(dt + 1) * P],
                         xT[i][z][:, kt, half * HALF:(half + 1) * HALF])
                        for kt in range(KT) for x, z in PARTS]
                for c, (l, r) in enumerate(todo):
                    last = nc.tensor.matmul(up_ps[t % 2][:], l, r, start=c == 0,
                                            stop=c == len(todo) - 1)
                last.then_inc(s["up_done"], 1)

            def down(e, i, t):
                k = e * STEPS + t
                half, dt = divmod(t, DT)
                if dt == 0:
                    after(pe, "y_b2", e * 4 + 2 * half - 2)
                after(pe, "h_lo", k + 1)
                for c in range(TB):
                    for n, (x, z) in enumerate(PARTS):
                        last = nc.tensor.matmul(
                            y_ps[half][c // 2][:, (c % 2) * M:(c % 2 + 1) * M],
                            hT[x][:, t % RING, c * P:(c + 1) * P], w2[i][z][:, dt, :],
                            start=dt == 0 and c % 2 == 0 and n == 0,
                            stop=dt == DT - 1 and c % 2 == 1 and n == 2)
                last.then_inc(s["down_done"], 1)

            write_list(0)
            for f in range(4):
                turn(0, 0, f)

            def body(e, i, more):
                for t in range(STEPS):
                    if t == 0:
                        after(pe, "e_xt_lo", 4 * e + 4)
                        after(pe, "w_lo2", 2 * e + 2)
                    up(e, i, t)
                    if t >= LAG:
                        down(e, i, t - LAG)
                    elif not (isinstance(e, int) and e == 0):
                        down(e - 1, 1 - i, STEPS + t - LAG)
                    if more and t == 2:
                        write_list(e + 1)
                    if more and 11 <= t < 15:
                        turn(e + 1, 1 - i, t - 11)
            experts(pe, body)
            for t in range(LAG):
                down(E - 1, 1, STEPS + t - LAG)


def build(nc, a):
    with (nc.sbuf_tensor("score", [P, E, NB], F32) as score,
          nc.sbuf_tensor("ident", [P, P], F32) as ident):
        with nc.sbuf_tensor("h2", [P, NB, M], F32) as h2:
            build_attention(nc, a, ident, h2)
            build_router(nc, a, ident, h2, score)
        build_experts(nc, a, ident, score)


def kernel(x, L0_tok_weight, L0_attn_w_aq, L0_attn_w_ak, L0_attn_w_av, L0_attn_w_ao,
           L0_ffn_Wr, L0_ffn_W1, L0_ffn_b1, L0_ffn_W2, L0_ffn_b2):
    import numpy as np
    import concourse.bacc as bacc
    from concourse.bass_utils import run_bass_kernel_spmd

    half = D // 2
    freqs = np.power(np.float32(10000.0), -np.arange(half, dtype=np.float32) / np.float32(half))
    angles = np.arange(T, dtype=np.float32)[None, :] * freqs[:, None].astype(np.float32)
    cos, sin = np.cos(angles), np.sin(angles)
    rope = np.stack([np.concatenate([cos, cos]), np.concatenate([-sin, sin])], 1)
    i = np.arange(P)
    later = i[None, :] > i[:, None]

    arrays = {
        "ids": np.ascontiguousarray(x.reshape(B, TB, P).transpose(0, 2, 1)),
        "emb": L0_tok_weight,
        "wq": L0_attn_w_aq.reshape(M, H * D), "wk": L0_attn_w_ak.reshape(M, H * D),
        "wv": L0_attn_w_av.reshape(M, H * D), "wo": L0_attn_w_ao,
        "wr": L0_ffn_Wr, "w1": L0_ffn_W1, "b1": L0_ffn_b1, "w2": L0_ffn_W2, "b2": L0_ffn_b2,
        "rope": rope.astype(np.float32), "ident": np.eye(P, dtype=np.float32),
        "mask": np.where(later, np.float32(1e30), np.float32(0)),
        "tri": later.astype(np.float32),
    }
    arrays = {k: np.ascontiguousarray(v) for k, v in arrays.items()}
    nc = bacc.Bacc("TRN2", target_bir_lowering=False, num_devices=1)
    a = {k: nc.dram_tensor(f"in_{k}", v.shape, mybir.dt.from_np(v.dtype), kind="ExternalInput").ap()
         for k, v in arrays.items()}
    a["out"] = nc.dram_tensor("out_0", (N, M), F32, kind="ExternalOutput").ap()
    a["rows"] = nc.dram_tensor("routed_rows", (N, ROW), F32, kind="Internal").ap()
    build(nc, a)
    r = run_bass_kernel_spmd(nc, [{f"in_{k}": v for k, v in arrays.items()}], core_ids=[0])
    return r.results[0]["out_0"].reshape(B, T, M)
```

```python
import concourse.bass as bass
from concourse import mybir
from concourse.alu_op_type import AluOpType as ALU
from contextlib import ExitStack

F32 = mybir.dt.float32
F32R = mybir.dt.float32r
BF16 = mybir.dt.bfloat16
I32 = mybir.dt.int32
ACT = mybir.ActivationFunctionType
AX = mybir.AxisListType

P = 128
B, T, M = 8, 512, 256
H, D = 8, 128
VOCAB = 8000
N = B * T
TB = T // P
KT = M // P
NB = N // P
E, DI, TOPK = 8, 1024, 1024
EPS = 1e-5

ROWS = [(3, 0, 0, 0), (2, 1, 0, 512), (0, 1, 384, 896), (1, 0, 0, 1024)]
P_COL = {ib: col for ib, _, _, col in ROWS}
ROW_AT = {ib: k for k, (ib, _, _, _) in enumerate(ROWS)}
P_COLS = sum((ib + 1) * P for ib in range(TB))
PT_COL = {0: 0, 1: 512, 2: 896, 3: 1152}
T_FILLS = [([(2, 2), (2, 3), (3, 3)], 896), ([(0, 0), (0, 1), (0, 2), (0, 3)], 0),
           ([(1, 1), (1, 2), (1, 3)], 512)]
V_SLOT = {0: [0, 1], 1: [2], 2: [3], 3: [4], 4: [5], 5: [6], 6: [7], 7: []}


def build_attention(nc, a, ident, h2):
    ctx = ExitStack()
    with ctx:
        def sb(name, shape, dt=F32):
            return ctx.enter_context(nc.sbuf_tensor(name, shape, dt))

        def sem(name):
            return ctx.enter_context(nc.semaphore(name))

        w_qkv = {k: [sb(f"w{k}_{p}", [P, KT, H * D], F32R) for p in ("hi", "lo")] for k in "qkv"}
        w_o = [sb(f"wo_{p}", [P, H, M], F32R) for p in ("hi", "lo")]
        rope_k = sb("rope_k", [P, 2, T])
        rope_q = sb("rope_q", [P, 2, T])
        ident_bf = sb("ident_bf", [P, P], BF16)
        mask_bf = sb("mask_bf", [P, P], BF16)
        mask_f = sb("mask_f", [P, P])
        neg_half = sb("neg_half", [P, TB])
        ids = sb("ids", [P, TB], I32)
        emb = sb("emb", [P, TB, M])
        emb_res = sb("emb_res", [P, TB, M])
        xn = sb("xn", [P, TB, M])
        stats = sb("stats", [P, TB, 6])
        mean_var = sb("mean_var", [P, TB, 2])
        rstd = sb("rstd", [P, TB])
        xT = [sb(f"xT_{p}", [P, KT, T], F32R) for p in ("hi", "lo")]
        q_cos, q_sin = sb("q_cos", [P, T]), sb("q_sin", [P, T])
        k_cos, k_sin = sb("k_cos", [P, T]), sb("k_sin", [P, T])
        qT = [sb(f"qT_{p}", [P, 2, T], F32R) for p in ("hi", "lo")]
        kT = [sb(f"kT_{p}", [P, 2, T], F32R) for p in ("hi", "lo")]
        v = [sb(f"v_{p}", [P, 2 * TB, 4 * D], F32R) for p in ("hi", "lo")]
        prob = sb("prob", [P, 2, P_COLS])
        row_min = sb("row_min", [P, 2, TB])
        row_sum = sb("row_sum", [P, 2, TB])
        row_inv = sb("row_inv", [P, 2, TB])
        pT = [sb(f"pT_{p}", [P, P_COLS], F32R) for p in ("hi", "lo")]
        oT = [sb(f"oT_{p}", [P, T], F32R) for p in ("hi", "lo")]

        bank = [ctx.enter_context(nc.psum_tensor(f"bank{i}", [P, 512], F32)) for i in range(8)]
        proj_ps, s_ps, r_ps = bank[0:2], bank[2:4], bank[6:8]
        o_ps, t_ps = bank[4], [bank[5], bank[4], bank[5]]

        names = """wq_in wk_in wv_in wo_in tables_in w_hi w_lo consts
            ids_in emb_in res_in stats_done aggr_done var_eps rstd_done xn_ready xt_tr xt_hi xt_lo
            q_proj k_proj v_proj q_rope k_rope q_add k_add q_hi k_hi q_lo k_lo v_hi v_lo
            s_done s_min exp_done inv_done norm_done t_done t_hi t_lo o_done o_hi o_lo
            out_done r_evac apart""".split()
        s = {n: sem(n) for n in names}

        block = ctx.enter_context(nc.Block())

        def after(eng, name, count):
            if isinstance(count, int) and count <= 0:
                return
            eng.wait_ge(s[name], count)

        def alone(eng):
            eng.sem_inc(s["apart"], 1)

        def batches(eng, body):
            body(0, range(8), lambda h: h >= 0)
            with eng.Fori(1, B - 1) as b:
                body(b, range(8), lambda h: True)
            body(B - 1, range(11), lambda h: h < H)

        wsrc = {k: a[f"w{k}"].rearrange("(t p) n -> p t n", p=P) for k in "qkv"}
        wraw = {k: h2[:, 8 * i:8 * i + 8, :].rearrange("p (t g) m -> p t (g m)", t=KT)
                for i, k in enumerate("qkv")}
        wraw_o = h2[:, 24:32, :]

        @block.sync
        def _(sp):
            sp.dma_start(ids[:], a["ids"][0]).then_inc(s["ids_in"], 16)
            sp.dma_start(ident[:], a["ident"][:, :]).then_inc(s["tables_in"], 16)
            sp.dma_start(mask_f[:], a["mask"][:, :]).then_inc(s["tables_in"], 16)
            sp.dma_start(rope_k[:], a["rope"][:, :, :]).then_inc(s["tables_in"], 16)
            for k in "qkv":
                sp.dma_start(wraw[k], wsrc[k]).then_inc(s[f"w{k}_in"], 16)
            sp.dma_start(wraw_o, a["wo"].rearrange("h d m -> d h m")).then_inc(s["wo_in"], 16)

            def body(b, slots, ok):
                after(sp, "r_evac", b)
                after(sp, "emb_in", (b + 1) * 16 * TB)
                sp.dma_start(emb_res[:], emb[:]).then_inc(s["res_in"], 16)
                if len(slots) == H:
                    sp.dma_start(ids[:], a["ids"][b + 1]).then_inc(s["ids_in"], 16)
            batches(sp, body)

        @block.gpsimd
        def _(pool):
            nc.gpsimd.memset(neg_half[:], -0.5).then_inc(s["consts"], 1)

            def gather(b, blocks):
                after(pool, "ids_in", (b + 1) * 16)
                after(pool, "res_in", b * 16)
                after(pool, "xn_ready", b)
                alone(pool)
                for tb in blocks:
                    pool.indirect_dma_start(emb[:, tb, :], None, a["emb"][:, :],
                                            bass.IndirectOffsetOnAxis(ids[:, tb:tb + 1], 0))\
                        .then_inc(s["emb_in"], 16)

            def rsqrt(b):
                after(pool, "aggr_done", b + 1)
                alone(pool)
                nc.gpsimd.tensor_scalar(rstd[:], mean_var[:, :, 1], EPS, None, ALU.add)\
                    .then_inc(s["var_eps"], 1)
                after(pool, "var_eps", b + 1)
                nc.gpsimd.tensor_tensor(rstd[:], rstd[:], neg_half[:], ALU.pow)\
                    .then_inc(s["rstd_done"], 1)

            def norm(b, h, ks):
                alone(pool)
                for k in ks:
                    ib, _, _, col = ROWS[k]
                    pr = prob[:, h % 2, col:col + (ib + 1) * P]
                    nc.gpsimd.tensor_scalar(pr, pr, row_inv[:, h % 2, k:k + 1], 1.0,
                                            ALU.mult, ALU.mult).then_inc(s["norm_done"], 1)

            def add(b, h, x):
                n = b * H + h
                cos, sin = (q_cos, q_sin) if x == "q" else (k_cos, k_sin)
                after(pool, f"{x}_rope", n + 1)
                nc.gpsimd.tensor_tensor(cos[:], cos[:], sin[:], ALU.add).then_inc(s[f"{x}_add"], 1)

            def low(b, h, x):
                n = b * H + h
                cos, out = (q_cos, qT) if x == "q" else (k_cos, kT)
                after(pool, f"{x}_hi", n + 1)
                nc.gpsimd.tensor_tensor(out[1][:, h % 2, :], cos[:], out[0][:, h % 2, :].bitcast(F32),
                                        ALU.subtract).then_inc(s[f"{x}_lo"], 1)

            pool.wait_ge(s["consts"], 1)
            gather(0, range(TB))
            rsqrt(0)

            def body(b, slots, ok):
                for h in slots:
                    n = b * H + h
                    live = ok(h) and h < H
                    if live:
                        add(b, h, "q")
                    if ok(h - 2):
                        after(pool, "inv_done", 2 * (n - 2) + 2)
                        norm(b, h - 2, [3])
                    if live:
                        low(b, h, "q")
                        add(b, h, "k")
                        low(b, h, "k")
                    if len(slots) == H and h in (3, 4, 5):
                        gather(b + 1, [h - 3])
                    if len(slots) == H and h == 6:
                        rsqrt(b + 1)
                    if ok(h - 1):
                        after(pool, "inv_done", 2 * (n - 1) + 1)
                        norm(b, h - 1, [0, 1, 2])
                    if len(slots) == H and h == 4:
                        gather(b + 1, [3])
            batches(pool, body)

        @block.scalar
        def _(act):
            def hi_of(out, in_, name):
                nc.scalar.activation(out, in_, ACT.Copy).then_inc(s[name], 1)

            act.wait_ge(s["tables_in"], 48)
            nc.scalar.activation(ident_bf[:], ident[:], ACT.Copy).then_inc(s["w_hi"], 1)
            nc.scalar.activation(mask_bf[:], mask_f[:], ACT.Copy).then_inc(s["w_hi"], 1)
            nc.scalar.activation(rope_q[:], rope_k[:], ACT.Copy, scale=-1.0 / D)\
                .then_inc(s["w_hi"], 1)

            def xt(b):
                for kt in range(KT):
                    after(act, "xt_tr", KT * b + kt + 1)
                    hi_of(xT[0][:, kt, :], proj_ps[kt][:], "xt_hi")

            def exp(b, h, k):
                n = b * H + h
                ib, bk, pc, col = ROWS[k]
                w = (ib + 1) * P
                after(act, "s_min", TB * n + (1, 3, 3, 4)[k])
                after(act, "t_done", 3 * (n - 2) + 3)
                nc.scalar.activation(prob[:, h % 2, col:col + w], s_ps[bk][:, pc:pc + w], ACT.Exp,
                                     bias=row_min[:, h % 2, k:k + 1], scale=-1.0,
                                     accum_out=row_sum[:, h % 2, k:k + 1]).then_inc(s["exp_done"], 1)

            def t_high(b, h, f):
                n = b * H + h
                pairs, col = T_FILLS[f]
                w = len(pairs) * P
                after(act, "t_done", 3 * n + f + 1)
                after(act, "o_done", n)
                hi_of(pT[0][:, col:col + w], t_ps[f][:, 0:w], "t_hi")

            def qk_high(b, h, x):
                n = b * H + h
                cos, out = (q_cos, qT) if x == "q" else (k_cos, kT)
                after(act, f"{x}_add", n + 1)
                after(act, "s_done", 3 * (n - 2) + 3)
                hi_of(out[0][:, h % 2, :], cos[:], f"{x}_hi")

            def v_high(b, h, i):
                t = V_SLOT[h][i]
                after(act, "v_proj", 2 * TB * b + t + 1)
                after(act, "o_done", (b - 1) * H + 4 * (t // TB) + 4)
                hi_of(v[0][:, t, :], proj_ps[i][:], "v_hi")

            for k in "qk":
                act.wait_ge(s[f"w{k}_in"], 16)
                hi_of(w_qkv[k][0][:], wraw[k], "w_hi")
            xt(0)
            act.wait_ge(s["wv_in"], 16)
            hi_of(w_qkv["v"][0][:], wraw["v"], "w_hi")
            act.wait_ge(s["wo_in"], 16)
            hi_of(w_o[0][:], wraw_o, "w_hi")

            def body(b, slots, ok):
                for h in slots:
                    n = b * H + h
                    live = ok(h) and h < H
                    if ok(h - 3):
                        after(act, "o_done", n - 3 + 1)
                        after(act, "out_done", n - 3)
                        hi_of(oT[0][:], o_ps[:], "o_hi")
                    if live:
                        qk_high(b, h, "q")
                    if ok(h - 2):
                        t_high(b, h - 2, 0)
                    if ok(h - 1):
                        exp(b, h - 1, 0)
                    if live:
                        for i in range(len(V_SLOT[h])):
                            v_high(b, h, i)
                        qk_high(b, h, "k")
                    if ok(h - 1):
                        exp(b, h - 1, 1)
                    if ok(h - 2):
                        t_high(b, h - 2, 1)
                    if ok(h - 1):
                        exp(b, h - 1, 2)
                    if len(slots) == H and h == 7:
                        xt(b + 1)
                    if ok(h - 2):
                        t_high(b, h - 2, 2)
                    if ok(h - 1):
                        exp(b, h - 1, 3)
            batches(act, body)

        @block.vector
        def _(dve):
            def low_of(out, in_, hi, name):
                nc.vector.tensor_tensor(out, in_, hi.bitcast(F32), ALU.subtract)\
                    .then_inc(s[name], 1)

            def stats_of(b):
                after(dve, "emb_in", (b + 1) * 16 * TB)
                for tb in range(TB):
                    nc.vector.bn_stats(stats[:, tb, :], emb[:, tb, :]).then_inc(s["stats_done"], 1)
                after(dve, "stats_done", TB * (b + 1))
                alone(dve)
                for tb in range(TB):
                    last = nc.vector.bn_aggr(mean_var[:, tb, :], stats[:, tb, :])
                last.then_inc(s["aggr_done"], 1)

            def normalise(b):
                after(dve, "rstd_done", b + 1)
                after(dve, "xt_tr", KT * b)
                for tb in range(TB):
                    last = nc.vector.tensor_scalar(xn[:, tb, :], emb[:, tb, :], mean_var[:, tb, 0:1],
                                                   rstd[:, tb:tb + 1], ALU.subtract, ALU.mult)
                last.then_inc(s["xn_ready"], 1)

            def xt(b):
                for kt in range(KT):
                    after(dve, "xt_hi", KT * b + kt + 1)
                    low_of(xT[1][:, kt, :], proj_ps[kt][:], xT[0][:, kt, :], "xt_lo")

            def rope(b, h, x):
                n = b * H + h
                ps, table, cos, sin = ((proj_ps[0], rope_q, q_cos, q_sin) if x == "q" else
                                       (proj_ps[1], rope_k, k_cos, k_sin))
                after(dve, f"{x}_proj", n + 1)
                after(dve, f"{x}_lo", n)
                nc.vector.tensor_tensor(cos[:], ps[:], table[:, 0, :], ALU.mult)
                nc.vector.tensor_tensor(sin[0:64, :], ps[64:128, :], table[0:64, 1, :], ALU.mult)
                nc.vector.tensor_tensor(sin[64:128, :], ps[0:64, :], table[64:128, 1, :], ALU.mult)\
                    .then_inc(s[f"{x}_rope"], 1)

            def t_low(b, h, f):
                n = b * H + h
                pairs, col = T_FILLS[f]
                w = len(pairs) * P
                after(dve, "t_hi", 3 * n + f + 1)
                low_of(pT[1][:, col:col + w], t_ps[f][:, 0:w], pT[0][:, col:col + w], "t_lo")

            def minimum(b, h, k):
                n = b * H + h
                ib, bk, pc, _ = ROWS[k]
                nc.vector.tensor_reduce(row_min[:, h % 2, k:k + 1], s_ps[bk][:, pc:pc + (ib + 1) * P],
                                        AX.X, ALU.min).then_inc(s["s_min"], 1)

            def inverse(b, h, lo, hi):
                nc.vector.reciprocal(row_inv[:, h % 2, lo:hi], row_sum[:, h % 2, lo:hi])\
                    .then_inc(s["inv_done"], 1)

            def evacuate(b):
                after(dve, "out_done", H * (b + 1))
                after(dve, "res_in", 16 * (b + 1))
                if isinstance(b, int) and b == 0:
                    dve.wait_ge(s["w_lo"], 4)
                for i in range(2):
                    last = nc.vector.tensor_tensor(
                        h2[:, bass.ds(b * TB + 2 * i, 2), :],
                        r_ps[i][:].rearrange("p (t m) -> p t m", m=M),
                        emb_res[:, 2 * i:2 * i + 2, :], ALU.add)
                last.then_inc(s["r_evac"], 1)

            stats_of(0)
            normalise(0)
            for i, k in enumerate("qk"):
                after(dve, "w_hi", 4 + i)
                low_of(w_qkv[k][1][:], wraw[k], w_qkv[k][0][:], "w_lo")
            xt(0)
            after(dve, "w_hi", 6)
            low_of(w_qkv["v"][1][:], wraw["v"], w_qkv["v"][0][:], "w_lo")
            after(dve, "w_hi", 7)
            low_of(w_o[1][:], wraw_o, w_o[0][:], "w_lo")

            def body(b, slots, ok):
                for h in slots:
                    n = b * H + h
                    live = ok(h) and h < H
                    if live:
                        rope(b, h, "q")
                    if ok(h - 2):
                        after(dve, "exp_done", TB * (n - 2) + 4)
                        inverse(b, h - 2, 3, 4)
                    if live:
                        rope(b, h, "k")
                    if ok(h - 3):
                        after(dve, "o_hi", n - 3 + 1)
                        low_of(oT[1][:], o_ps[:], oT[0][:], "o_lo")
                    if len(slots) == H and h == 6:
                        stats_of(b + 1)
                    if ok(h - 2):
                        t_low(b, h - 2, 0)
                    if ok(h - 1):
                        after(dve, "s_done", 3 * (n - 1) + 1)
                        minimum(b, h - 1, 0)
                        after(dve, "s_done", 3 * (n - 1) + 2)
                        minimum(b, h - 1, 1)
                        minimum(b, h - 1, 2)
                    if live:
                        for i, t in enumerate(V_SLOT[h]):
                            after(dve, "v_hi", 2 * TB * b + t + 1)
                            low_of(v[1][:, t, :], proj_ps[i][:], v[0][:, t, :], "v_lo")
                    if ok(h - 2):
                        t_low(b, h - 2, 1)
                    if len(slots) == H and h == 7:
                        xt(b + 1)
                    if ok(h - 1):
                        after(dve, "s_done", 3 * (n - 1) + 3)
                        minimum(b, h - 1, 3)
                    if ok(h - 2):
                        t_low(b, h - 2, 2)
                    if ok(h - 1):
                        after(dve, "exp_done", TB * (n - 1) + 3)
                        inverse(b, h - 1, 0, 3)
                    if h == 2 and ok(h - 3):
                        evacuate(b - 1)
                    if h == 10:
                        evacuate(b)
                    if len(slots) == H and h == 6:
                        normalise(b + 1)
            batches(dve, body)

        @block.tensor
        def _(pe):
            PARTS = [(0, 0), (0, 1), (1, 0)]

            def products(out, pairs, start=True, stop=True):
                todo = [(l[i], r[j]) for l, r in pairs for i, j in PARTS]
                for c, (l, r) in enumerate(todo):
                    last = nc.tensor.matmul(out, l, r, start=start and c == 0,
                                            stop=stop and c == len(todo) - 1)
                return last

            def xt(b):
                after(pe, "xn_ready", b + 1)
                for kt in range(KT):
                    after(pe, "k_rope" if kt else "q_rope", b * H)
                    for tb in range(TB):
                        last = nc.tensor.transpose(proj_ps[kt][:, tb * P:(tb + 1) * P],
                                                   xn[:, tb, kt * P:(kt + 1) * P], ident[:])
                    last.then_inc(s["xt_tr"], 1)

            def project(b, h, x):
                n = b * H + h
                ps = proj_ps[0 if x == "q" else 1]
                if h == 0:
                    after(pe, "xt_lo", KT * (b + 1))
                elif x == "q":
                    after(pe, "v_lo", 2 * TB * b + V_SLOT[h - 1][-1] + 1)
                elif h == 1:
                    after(pe, "v_lo", 2 * TB * b + 2)
                else:
                    after(pe, "k_rope", n)
                products(ps[:], [([w[:, kt, h * D:(h + 1) * D] for w in w_qkv[x]],
                                  [t[:, kt, :] for t in xT]) for kt in range(KT)])\
                    .then_inc(s[f"{x}_proj"], 1)

            def values(b, h, i):
                n = b * H + h
                g, jb = divmod(V_SLOT[h][i], TB)
                after(pe, "k_rope" if i else "q_rope", n + 1)
                products(proj_ps[i][:], [([t[:, kt, jb * P:(jb + 1) * P] for t in xT],
                                          [w[:, kt, g * 512:(g + 1) * 512] for w in w_qkv["v"]])
                                         for kt in range(KT)]).then_inc(s["v_proj"], 1)

            def scores(b, h, ks):
                n = b * H + h
                for k in ks:
                    ib, bk, pc, _ = ROWS[k]
                    w = (ib + 1) * P
                    products(s_ps[bk][:, pc:pc + w],
                             [([q[:, h % 2, ib * P:(ib + 1) * P] for q in qT],
                               [x[:, h % 2, 0:w] for x in kT])], stop=False)
                    last = nc.tensor.matmul(s_ps[bk][:, pc + ib * P:pc + w], ident_bf[:], mask_bf[:],
                                            start=False, stop=True)
                last.then_inc(s["s_done"], 1)

            def turn(b, h, f):
                n = b * H + h
                after(pe, "o_lo" if f == 1 else "t_lo", n if f == 1 else 3 * n + f // 2)
                for c, (jb, ib) in enumerate(T_FILLS[f][0]):
                    col = P_COL[ib] + jb * P
                    last = nc.tensor.transpose(t_ps[f][:, c * P:(c + 1) * P],
                                               prob[:, h % 2, col:col + P], ident[:])
                last.then_inc(s["t_done"], 1)

            def weigh(b, h):
                n = b * H + h
                g = (h % H) // 4
                after(pe, "t_lo", 3 * n + 2)
                after(pe, "v_lo", 2 * TB * b + TB * (g + 1) if 0 <= h < H
                      else 2 * TB * (b - 1) + TB * (g + 1))
                order = [0, 2, 3, 1]
                for jb in order:
                    if jb == order[-1]:
                        after(pe, "t_lo", 3 * n + 3)
                    w = T - jb * P
                    c = (h % 4) * D
                    last = products(o_ps[:, jb * P:T],
                                    [([x[:, g * TB + jb, c:c + D] for x in v],
                                      [x[:, PT_COL[jb]:PT_COL[jb] + w] for x in pT])],
                                    start=jb == 0, stop=jb == order[-1])
                last.then_inc(s["o_done"], 1)

            def output(b, h, half):
                n = b * H + h
                hh = h % H
                after(pe, "o_lo", n + 1)
                if hh == 0:
                    after(pe, "r_evac", b if h >= 0 else b - 1)
                for ib in (2 * half, 2 * half + 1):
                    last = products(r_ps[half][:, (ib % 2) * M:(ib % 2 + 1) * M],
                                    [([x[:, ib * P:(ib + 1) * P] for x in oT],
                                      [w[:, hh, :] for w in w_o])],
                                    start=hh == 0 and ib % 2 == 0,
                                    stop=hh == H - 1 and ib % 2 == 1)
                if half:
                    last.then_inc(s["out_done"], 1)

            pe.wait_ge(s["tables_in"], 48)
            xt(0)

            def body(b, slots, ok):
                for h in slots:
                    n = b * H + h
                    live = ok(h) and h < H
                    if live:
                        if isinstance(b, int) and b == 0 and h == 0:
                            pe.wait_ge(s["w_lo"], 1)
                        project(b, h, "q")
                        if isinstance(b, int) and b == 0 and h == 0:
                            pe.wait_ge(s["w_lo"], 2)
                        project(b, h, "k")
                    if ok(h - 3):
                        weigh(b, h - 3)
                    if ok(h - 2):
                        after(pe, "norm_done", TB * (n - 2) + 2)
                        turn(b, h - 2, 0)
                    if ok(h - 1):
                        after(pe, "q_lo", n)
                        after(pe, "k_lo", n)
                        after(pe, "exp_done", TB * (n - 1))
                        scores(b, h - 1, [0])
                        after(pe, "exp_done", TB * (n - 2) + 3)
                        scores(b, h - 1, [1, 2])
                    if live:
                        if isinstance(b, int) and b == 0 and h == 0:
                            pe.wait_ge(s["w_lo"], 4)
                        for i in range(len(V_SLOT[h])):
                            values(b, h, i)
                    if ok(h - 3):
                        output(b, h - 3, 0)
                    if ok(h - 2):
                        after(pe, "norm_done", TB * (n - 2) + 4)
                        turn(b, h - 2, 1)
                    if len(slots) == H and h == 7:
                        xt(b + 1)
                    if ok(h - 3):
                        output(b, h - 3, 1)
                    if ok(h - 1):
                        after(pe, "exp_done", TB * (n - 1) + 1)
                        scores(b, h - 1, [3])
                    if ok(h - 2):
                        turn(b, h - 2, 2)
            batches(pe, body)
LIST_A = 32
CH = TOPK // P
HALF = 512
DT = DI // P
ROW = M + E


def build_router(nc, a, ident, h2, score):
    ctx = ExitStack()
    with ctx:
        def sb(name, shape, dt=F32):
            return ctx.enter_context(nc.sbuf_tensor(name, shape, dt))

        rows = sb("rows", [P, NB, ROW])
        wr = sb("wr", [P, KT, E])
        stats = sb("r_stats", [P, NB, 6])
        mean_var = sb("r_mean_var", [P, NB, 2])
        rstd = sb("r_rstd", [P, NB])
        neg_half = sb("r_neg_half", [P, NB])
        xT = sb("r_xT", [P, 4, KT, P])
        top = sb("r_top", [P, NB])
        total = sb("r_total", [P, NB])
        logit = sb("r_logit", [P, NB, E])
        x_ps = [ctx.enter_context(nc.psum_tensor(f"rx{i}", [P, 512], F32)) for i in range(4)]
        l_ps = ctx.enter_context(nc.psum_tensor("r_logits", [P, NB, E], F32))
        names = """r_in h2_out rows_out r_const r_stats_done r_aggr r_eps r_rstd_done r_norm
            r_tr r_copy r_logits_done r_step r_exp r_score""".split()
        s = {n: ctx.enter_context(nc.semaphore(n)) for n in names}
        block = ctx.enter_context(nc.Block())

        @block.sync
        def _(sp):
            sp.dma_start(wr[:], a["wr"].rearrange("(t p) e -> p t e", p=P)).then_inc(s["r_in"], 16)
            sp.dma_start(a["out"].rearrange("(b p) m -> p b m", p=P), h2[:]).then_inc(s["h2_out"], 16)
            sp.wait_ge(s["r_score"], 2)
            sp.dma_start(a["rows"].rearrange("(b p) m -> p b m", p=P), rows[:])\
                .then_inc(s["rows_out"], 16)
            sp.wait_ge(s["h2_out"], 16)
            sp.wait_ge(s["rows_out"], 16)

        @block.gpsimd
        def _(pool):
            nc.gpsimd.memset(neg_half[:], -0.5).then_inc(s["r_const"], 1)
            pool.wait_ge(s["r_const"], 1)
            pool.wait_ge(s["r_aggr"], NB)
            nc.gpsimd.tensor_scalar(rstd[:], mean_var[:, :, 1], EPS, None, ALU.add)\
                .then_inc(s["r_eps"], 1)
            pool.wait_ge(s["r_eps"], 1)
            nc.gpsimd.tensor_tensor(rstd[:], rstd[:], neg_half[:], ALU.pow)\
                .then_inc(s["r_rstd_done"], 1)

        @block.vector
        def _(dve):
            step = [0]

            def chained(ins):
                step[0] += 1
                ins.then_inc(s["r_step"], 1)
                dve.wait_ge(s["r_step"], step[0])

            for t in range(NB):
                nc.vector.bn_stats(stats[:, t, :], h2[:, t, :]).then_inc(s["r_stats_done"], 1)
            for t in range(NB):
                dve.wait_ge(s["r_stats_done"], t + 1)
                nc.vector.bn_aggr(mean_var[:, t, :], stats[:, t, :]).then_inc(s["r_aggr"], 1)
            dve.wait_ge(s["r_rstd_done"], 1)
            for t in range(NB):
                nc.vector.tensor_scalar(rows[:, t, 0:M], h2[:, t, :], mean_var[:, t, 0:1],
                                        rstd[:, t:t + 1], ALU.subtract, ALU.mult)\
                    .then_inc(s["r_norm"], 1)
            dve.wait_ge(s["r_logits_done"], NB)
            chained(nc.vector.tensor_reduce(top[:], l_ps[:], AX.X, ALU.max))
            nc.vector.tensor_tensor(logit[:], l_ps[:], top[:].unsqueeze(2).to_broadcast([P, NB, E]),
                                    ALU.subtract).then_inc(s["r_exp"], 1)
            dve.wait_ge(s["r_exp"], 2)
            chained(nc.vector.tensor_reduce(total[:], logit[:], AX.X, ALU.add))
            chained(nc.vector.reciprocal(total[:], total[:]))
            nc.vector.tensor_tensor(rows[:, :, M:ROW], logit[:],
                                    total[:].unsqueeze(2).to_broadcast([P, NB, E]), ALU.mult)\
                .then_inc(s["r_score"], 1)
            nc.vector.tensor_tensor(score[:].rearrange("p e b -> p b e"), logit[:],
                                    total[:].unsqueeze(2).to_broadcast([P, NB, E]), ALU.mult)\
                .then_inc(s["r_score"], 1)

        @block.scalar
        def _(act):
            for t in range(NB):
                act.wait_ge(s["r_tr"], t + 1)
                if t >= 4:
                    act.wait_ge(s["r_logits_done"], t - 3)
                nc.scalar.activation(xT[:, t % 4, :, :].rearrange("p k n -> p (k n)"),
                                     x_ps[t % 4][:, 0:KT * P], ACT.Copy).then_inc(s["r_copy"], 1)
            act.wait_ge(s["r_exp"], 1)
            nc.scalar.activation(logit[:], logit[:], ACT.Exp).then_inc(s["r_exp"], 1)

        @block.tensor
        def _(pe):
            pe.wait_ge(s["r_in"], 16)
            for t in range(NB + 2):
                if t < NB:
                    pe.wait_ge(s["r_norm"], t + 1)
                    if t >= 4:
                        pe.wait_ge(s["r_copy"], t - 3)
                    for kt in range(KT):
                        last = nc.tensor.transpose(x_ps[t % 4][:, kt * P:(kt + 1) * P],
                                                   rows[:, t, kt * P:(kt + 1) * P], ident[:])
                    last.then_inc(s["r_tr"], 1)
                if t >= 2:
                    u = t - 2
                    pe.wait_ge(s["r_copy"], u + 1)
                    for kt in range(KT):
                        last = nc.tensor.matmul(l_ps[:, u, :], xT[:, u % 4, kt, :], wr[:, kt, :],
                                                start=kt == 0, stop=kt == KT - 1)
                    last.then_inc(s["r_logits_done"], 1)


def build_experts(nc, a, ident, score):
    ctx = ExitStack()
    with ctx:
        def sb(name, shape, dt=F32):
            return ctx.enter_context(nc.sbuf_tensor(name, shape, dt))

        def ps(name, shape=(P, 512)):
            return ctx.enter_context(nc.psum_tensor(name, list(shape), F32))

        groups_f, groups = sb("groups_f", [P, 2, P]), sb("groups", [P, 2, P], BF16)
        EH = 2
        scoreT = sb("scoreT", [P, EH, P])
        least = sb("least", [P, EH], I32)
        step_bits = sb("step_bits", [P, 3, EH], I32)
        step_f = sb("step_f", [P, EH])
        cand = sb("cand", [P, 3, EH], I32)
        hits = sb("hits", [P, 3, EH, P], BF16)
        count_bf = sb("count_bf", [P, 3, EH], BF16)
        enough = sb("enough", [P, 3, EH])
        steps = sb("steps", [P, EH])
        steps_i = sb("steps_i", [P, EH], I32)
        above, equal = sb("above", [P, EH, P]), sb("equal", [P, EH, P])
        chosen = sb("chosen", [P, EH, P])
        need = sb("need", [P, EH])
        base = sb("base", [P, EH])
        rank = sb("rank", [P, EH, P])
        all_ones = sb("all_ones", [P, P])
        place = sb("place", [P, E, NB], I32)
        place_a, place_b = sb("place_a", [P, E, NB], I32), sb("place_b", [P, E, NB], I32)
        at_a, at_b = sb("at_a", [P, E, NB], BF16), sb("at_b", [P, E, NB], BF16)
        iota_i = sb("iota_i", [P, LIST_A], I32)
        iota32 = sb("iota32", [P, LIST_A], BF16)
        blk_i = sb("blk_i", [P, NB], I32)
        blk_no = sb("blk_no", [P, NB], BF16)
        tok_i = sb("tok_i", [P, 1], I32)
        tok_no = sb("tok_no", [P, 1])
        hot_a = sb("hot_a", [P, NB, LIST_A], BF16)
        hot_b = sb("hot_b", [P, NB, 3, LIST_A], BF16)
        list_tok = sb("list_tok", [LIST_A, LIST_A])
        list_f = sb("list_f", [LIST_A, LIST_A])
        tokens = [sb(f"tokens{i}", [P, CH], I32) for i in range(2)]
        raw1, raw2 = sb("raw1", [P, KT, DI]), sb("raw2", [P, DT, M])
        w1 = [[sb(f"w1_{i}{p}", [P, KT, DI], F32R) for p in ("hi", "lo")] for i in range(2)]
        w2 = [[sb(f"w2_{i}{p}", [P, DT, M], F32R) for p in ("hi", "lo")] for i in range(2)]
        b1_rows = sb("b1_rows", [E * DT, P])
        b1 = sb("b1", [P, E * DT])
        b1_e = [sb(f"b1_e{i}", [P, DT]) for i in range(2)]
        b2 = sb("b2", [P, E, M])
        got = [sb(f"got{i}", [P, CH, ROW]) for i in range(2)]
        gate = [sb(f"gate{i}", [P, CH]) for i in range(2)]
        xT = [[sb(f"e_xT{i}{p}", [P, KT, TOPK], F32R) for p in ("hi", "lo")] for i in range(2)]
        hid = sb("hid", [P, 2, HALF])
        hT = [sb(f"hT_{p}", [P, 4, HALF], F32R) for p in ("hi", "lo")]
        y = [sb(f"y{i}", [P, TB, M]) for i in range(2)]

        up_ps = [ps("up0"), ps("up1")]
        y_ps = [[ps("y00"), ps("y01")], [ps("y10"), ps("y11")]]
        x_ps, l_ps = ps("x_ps"), ps("l_ps")

        names = """c_in b2_in c_const c_step counted totalled marked ranked turned b1_tr b1_ready
            raw_in w_hi2 w_lo2 up_done down_done h_hi h_lo e_xt_tr e_xt_hi e_xt_lo hot_ready listed
            tok_ready rows_in0 rows_in1 gate_ready y_b2 y_gated added0 added1 l_chain e_apart""".split()
        s = {n: ctx.enter_context(nc.semaphore(n)) for n in names}
        block = ctx.enter_context(nc.Block())

        def after(eng, name, count):
            if isinstance(count, int) and count <= 0:
                return
            eng.wait_ge(s[name], count)

        def alone(eng):
            eng.sem_inc(s["e_apart"], 1)

        STEPS = 2 * DT
        RING = 4
        ITERATIONS = 15
        LAG = 2

        def experts(eng, body):
            for i in range(2):
                body(i, i, True)
            with eng.Fori(1, E // 2 - 1) as j:
                for i in range(2):
                    body(j * 2 + i, i, True)
            for i in range(2):
                body(E - 2 + i, i, i == 0)

        def wide(x):
            return x.unsqueeze(2).to_broadcast([P, E, NB])

        @block.sync
        def _(sp):
            sp.dma_start(groups_f[:], a["groups"][:, :, :]).then_inc(s["c_in"], 16)
            sp.dma_start(b1_rows[:], a["b1"].rearrange("e (t p) -> (e t) p", p=P))\
                .then_inc(s["c_in"], 16)
            sp.dma_start(b2[:], a["b2"].rearrange("(o e) m -> o e m", o=1).to_broadcast([P, E, M]))\
                .then_inc(s["b2_in"], 16)

            def load(e):
                after(sp, "w_lo2", 2 * e)
                sp.dma_start(raw1[:], a["w1"][e].rearrange("(t p) n -> p t n", p=P))\
                    .then_inc(s["raw_in"], 16)
                sp.dma_start(raw2[:], a["w2"][e].rearrange("(t p) m -> p t m", p=P))\
                    .then_inc(s["raw_in"], 16)
            load(0)
            experts(sp, lambda e, i, more: load(e + 1) if more else None)
            for half in range(2):
                sp.wait_ge(s[f"added{half}"], 16 * TB * E)

        @block.gpsimd
        def _(pool):
            nc.gpsimd.iota(iota_i[:], [[1, LIST_A]], base=0, channel_multiplier=0)\
                .then_inc(s["c_const"], 1)
            nc.gpsimd.iota(blk_i[:], [[1, NB]], base=0, channel_multiplier=0)\
                .then_inc(s["c_const"], 1)
            nc.gpsimd.iota(tok_i[:], [[1, 1]], base=0, channel_multiplier=1)\
                .then_inc(s["c_const"], 1)
            nc.gpsimd.memset(all_ones[:], 1.0).then_inc(s["c_const"], 1)
            nc.gpsimd.memset(least[:], 0).then_inc(s["c_const"], 1)
            nc.gpsimd.memset(step_f[:], float(1 << 28)).then_inc(s["c_const"], 1)
            for k in range(3):
                nc.gpsimd.memset(step_bits[:, k, :], (k + 1) << 28).then_inc(s["c_const"], 1)

            def gather(e, i):
                after(pool, "tok_ready", e + 1)
                after(pool, "e_xt_tr", 4 * (e - 1))
                after(pool, "gate_ready", e - 1)
                alone(pool)
                for c in range(CH):
                    pool.indirect_dma_start(got[i][:, c, :], None, a["rows"][:, :],
                                            bass.IndirectOffsetOnAxis(tokens[i][:, c:c + 1], 0))\
                        .then_inc(s[f"rows_in{c // TB}"], 16)

            def add(e, i, half):
                u = 2 * e + half
                after(pool, "gate_ready", e + 1)
                after(pool, "y_b2", 2 * u + 2)
                alone(pool)
                for c in range(TB):
                    nc.gpsimd.tensor_scalar(y[half][:, c, :], y[half][:, c, :],
                                            gate[i][:, TB * half + c:TB * half + c + 1], 1.0,
                                            ALU.mult, ALU.mult).then_inc(s["y_gated"], 1)
                if half == 0:
                    for k in range(2):
                        after(pool, f"added{k}", 16 * TB * e)
                for c in range(TB):
                    after(pool, "y_gated", TB * u + c + 1)
                    alone(pool)
                    pool.indirect_dma_start(a["out"][:, :],
                                            bass.IndirectOffsetOnAxis(
                                                tokens[i][:, TB * half + c:TB * half + c + 1], 0),
                                            y[half][:, c, :], None, compute_op=ALU.add)\
                        .then_inc(s[f"added{half}"], 16)

            gather(0, 0)

            def body(e, i, more):
                if not (isinstance(e, int) and e == 0):
                    add(e - 1, 1 - i, 1)
                if more:
                    gather(e + 1, 1 - i)
                add(e, i, 0)
            experts(pool, body)
            add(E - 1, 1, 1)

        @block.vector
        def _(dve):
            step = [0]

            def chained(ins):
                step[0] += 1
                ins.then_inc(s["c_step"], 1)
                dve.wait_ge(s["c_step"], step[0])

            dve.wait_ge(s["c_in"], 32)
            dve.wait_ge(s["c_const"], 9)
            nc.vector.tensor_copy(groups[:], groups_f[:])
            nc.vector.tensor_copy(iota32[:], iota_i[:]).then_inc(s["l_chain"], 1)
            nc.vector.tensor_copy(blk_no[:], blk_i[:])
            chained(nc.vector.tensor_copy(tok_no[:], tok_i[:]))
            dve.wait_ge(s["b1_tr"], 1)
            nc.vector.tensor_copy(b1[:], l_ps[:, 0:E * DT]).then_inc(s["b1_ready"], 1)

            dve.wait_ge(s["turned"], 1)
            chained(nc.vector.tensor_copy(scoreT[:].rearrange("p g t -> p (g t)"),
                                          x_ps[:, 0:EH * P]))

            with dve.Fori(0, ITERATIONS) as r:
                dve.wait_ge(s["l_chain"], r * 5 + 1)
                nc.vector.tensor_tensor(cand[:], step_bits[:],
                                        least[:].unsqueeze(1).to_broadcast([P, 3, EH]),
                                        ALU.bitwise_or).then_inc(s["l_chain"], 1)
                dve.wait_ge(s["l_chain"], r * 5 + 2)
                with nc.allow_low_precision(reason="counts up to 128 are exact in bfloat16"):
                    for k in range(3):
                        for g in range(EH):
                            last = nc.vector.tensor_scalar(
                                hits[:, k, g, :], scoreT[:, g, :],
                                cand[:, k, g:g + 1].bitcast(F32), None, ALU.is_ge, ALU.add,
                                accum_out=count_bf[:, k, g:g + 1])
                last.then_inc(s["counted"], 1)
                nc.vector.tensor_scalar(step_bits[:], step_bits[:], 2, None,
                                        ALU.logical_shift_right)
                dve.wait_ge(s["totalled"], r + 1)
                nc.vector.tensor_scalar(enough[:].rearrange("p k g -> p (k g)"), l_ps[:, 0:3 * EH],
                                        float(TOPK), None, ALU.is_ge).then_inc(s["l_chain"], 1)
                dve.wait_ge(s["l_chain"], r * 5 + 3)
                nc.vector.tensor_reduce(steps[:], enough[:].rearrange("p k g -> p g k"), AX.X,
                                        ALU.add).then_inc(s["l_chain"], 1)
                dve.wait_ge(s["l_chain"], r * 5 + 4)
                nc.vector.tensor_tensor(steps_i[:], steps[:], step_f[:], ALU.mult)\
                    .then_inc(s["l_chain"], 1)
                dve.wait_ge(s["l_chain"], r * 5 + 5)
                nc.vector.tensor_scalar(step_f[:], step_f[:], 0.25, None, ALU.mult)
                nc.vector.tensor_tensor(least[:], least[:], steps_i[:], ALU.bitwise_or)\
                    .then_inc(s["l_chain"], 1)
            dve.wait_ge(s["l_chain"], ITERATIONS * 5 + 1)

            def mark(out, op):
                with nc.allow_low_precision(reason="counts up to 128 are exact in bfloat16"):
                    for g in range(EH):
                        last = nc.vector.tensor_scalar(out[:, g, :], scoreT[:, g, :],
                                                       least[:, g:g + 1].bitcast(F32), None,
                                                       op, ALU.add, accum_out=count_bf[:, 0, g:g + 1])
                return last

            def ranks(marks, k):
                dve.wait_ge(s["ranked"], k)
                chained(nc.vector.tensor_copy(base[:], l_ps[:, 0:EH]))
                for g in range(EH):
                    last = nc.vector.tensor_tensor_scan(rank[:, g, :], all_ones[:], marks[:, g, :],
                                                        base[:, g:g + 1], ALU.mult, ALU.add)
                chained(last)

            mark(above, ALU.is_gt).then_inc(s["counted"], 1)
            dve.wait_ge(s["totalled"], ITERATIONS + 1)
            chained(nc.vector.tensor_scalar(need[:], l_ps[:, 0:EH], -1.0, float(TOPK),
                                            ALU.mult, ALU.add))
            mark(equal, ALU.is_equal).then_inc(s["marked"], 1)
            ranks(equal, 1)
            for g in range(EH):
                last = nc.vector.scalar_tensor_tensor(chosen[:, g, :], rank[:, g, :],
                                                      need[:, g:g + 1], equal[:, g, :],
                                                      ALU.is_le, ALU.mult)
            chained(last)
            chained(nc.vector.tensor_tensor(chosen[:], chosen[:], above[:], ALU.add))
            with nc.allow_low_precision(reason="counts up to 128 are exact in bfloat16"):
                nc.vector.tensor_reduce(count_bf[:, 0, :], chosen[:], AX.X, ALU.add)\
                    .then_inc(s["marked"], 1)
            ranks(chosen, 2)
            nc.vector.scalar_tensor_tensor(rank[:], chosen[:], -4.0 * TOPK, rank[:],
                                           ALU.mult, ALU.add).then_inc(s["marked"], 1)
            dve.wait_ge(s["turned"], 2)
            chained(nc.vector.tensor_scalar(place[:].rearrange("p e b -> p (e b)"),
                                            x_ps[:, 0:E * NB], 4.0 * TOPK - 1.0, None, ALU.add))
            chained(nc.vector.tensor_scalar(place_a[:], place[:], 5, None, ALU.logical_shift_right))
            chained(nc.vector.tensor_scalar(place_b[:], place[:], LIST_A - 1, None, ALU.bitwise_and))
            nc.vector.tensor_copy(at_a[:], place_a[:])
            chained(nc.vector.tensor_copy(at_b[:], place_b[:]))

            chain0 = ITERATIONS * 5 + 1

            def one_hots(e):
                after(dve, "listed", e)
                wide_iota = iota32[:].unsqueeze(1).to_broadcast([P, NB, LIST_A])

                def spread(x):
                    return x[:, bass.ds(e, 1), :].rearrange("p o b -> p (o b)").unsqueeze(2)\
                        .to_broadcast([P, NB, LIST_A])
                nc.vector.tensor_tensor(hot_a[:], spread(at_a), wide_iota, ALU.is_equal)
                nc.vector.tensor_tensor(hot_b[:, :, 0, :], spread(at_b), wide_iota, ALU.is_equal)\
                    .then_inc(s["l_chain"], 1)
                dve.wait_ge(s["l_chain"], e * 3 + (chain0 + 1))
                nc.vector.tensor_scalar(hot_b[:, :, 1, :], hot_b[:, :, 0, :], tok_no[:, 0:1], None,
                                        ALU.mult)
                nc.vector.tensor_tensor(hot_b[:, :, 2, :], hot_b[:, :, 0, :],
                                        blk_no[:].unsqueeze(2).to_broadcast([P, NB, LIST_A]),
                                        ALU.mult).then_inc(s["hot_ready"], 1)

            def write_list(e, i):
                after(dve, "listed", e + 1)
                for k in range(2):
                    after(dve, f"added{k}", 16 * TB * (e - 1))
                nc.vector.tensor_copy(list_tok[:], l_ps[0:LIST_A, 0:LIST_A]).then_inc(s["l_chain"], 1)
                dve.wait_ge(s["l_chain"], e * 3 + (chain0 + 2))
                nc.vector.scalar_tensor_tensor(list_f[:], l_ps[0:LIST_A, LIST_A:2 * LIST_A], float(P),
                                               list_tok[:], ALU.mult, ALU.add)\
                    .then_inc(s["l_chain"], 1)
                dve.wait_ge(s["l_chain"], e * 3 + (chain0 + 3))
                for q in range(P // LIST_A):
                    last = nc.vector.tensor_copy(
                        tokens[i][q * LIST_A:(q + 1) * LIST_A, :],
                        list_f[:].rearrange("a (c q) -> a q c", q=P // LIST_A)[:, q, :])
                last.then_inc(s["tok_ready"], 1)

            def low(out, in_, hi, name):
                nc.vector.tensor_tensor(out, in_, hi.bitcast(F32), ALU.subtract)\
                    .then_inc(s[name], 1)

            def split_weights(e, i, which):
                raw, w = ((raw1, w1), (raw2, w2))[which]
                after(dve, "w_hi2", 2 * e + which + 1)
                low(w[i][1][:], raw[:], w[i][0][:], "w_lo2")

            def first_bias(e, i):
                after(dve, "b1_ready", e + 1)
                after(dve, "h_hi", STEPS * (e - 1))
                nc.vector.tensor_scalar(b1_e[i][:], b1[:, bass.ds(e * DT, DT)], 1.0, None, ALU.mult)\
                    .then_inc(s["b1_ready"], 1)

            def gates(e, i):
                for half in range(2):
                    after(dve, f"rows_in{half}", 16 * TB * (e + 1))
                after(dve, "y_gated", CH * (e - 1))
                nc.vector.tensor_scalar(gate[i][:],
                                        got[i][:, :, bass.ds(e + M, 1)].rearrange("p c o -> p (c o)"),
                                        1.0, None, ALU.mult).then_inc(s["gate_ready"], 1)

            def xt_low(e, i, f):
                g, kt = divmod(f, 2)
                after(dve, "e_xt_hi", 4 * e + f + 1)
                cols = slice(g * HALF, (g + 1) * HALF)
                low(xT[i][1][:, kt, cols], x_ps[:], xT[i][0][:, kt, cols], "e_xt_lo")

            def results(e, half):
                u = 2 * e + half
                after(dve, "down_done", DT * (u + 1))
                after(dve, f"added{half}", 16 * TB * e)
                for k in range(2):
                    nc.vector.tensor_tensor(
                        y[half][:, 2 * k:2 * k + 2, :],
                        y_ps[half][k][:].rearrange("p (c m) -> p c m", m=M),
                        b2[:, bass.ds(e, 1), :].to_broadcast([P, 2, M]), ALU.add)\
                        .then_inc(s["y_b2"], 1)

            dve.wait_ge(s["b2_in"], 16)
            one_hots(0)
            write_list(0, 0)
            first_bias(0, 0)
            split_weights(0, 0, 0)
            split_weights(0, 0, 1)
            for f in range(2):
                xt_low(0, 0, f)

            def body(e, i, more):
                for t in range(STEPS):
                    k = e * STEPS + t
                    if more and t >= 12:
                        xt_low(e + 1, 1 - i, t - 12)
                    if more and t == 15:
                        gates(e + 1, 1 - i)
                    if isinstance(e, int) and e == 0 and t in (3, 4):
                        xt_low(0, 0, t - 1)
                    if isinstance(e, int) and e == 0 and t == 4:
                        gates(0, 0)
                    after(dve, "h_hi", k + 1)
                    low(hT[1][:, t % RING, :], hid[:, t % 2, :],
                        hT[0][:, t % RING, :], "h_lo")
                    if t == LAG and not (isinstance(e, int) and e == 0):
                        results(e - 1, 1)
                    if t == DT + LAG:
                        results(e, 0)
                    if more:
                        if t == 0:
                            one_hots(e + 1)
                        if t == 5:
                            write_list(e + 1, 1 - i)
                            first_bias(e + 1, 1 - i)
                        if t in (6, 8):
                            split_weights(e + 1, 1 - i, (t - 6) // 2)
            experts(dve, body)
            results(E - 1, 1)

        @block.scalar
        def _(act):
            def hi_of(out, in_, name):
                nc.scalar.activation(out, in_, ACT.Copy).then_inc(s[name], 1)

            def split_weights(e, i, which):
                raw, w = ((raw1, w1), (raw2, w2))[which]
                after(act, "raw_in", 32 * (e + 1))
                after(act, "down_done", STEPS * (e - 1))
                hi_of(w[i][0][:], raw[:], "w_hi2")

            def xt_high(e, i, f):
                g, kt = divmod(f, 2)
                after(act, "e_xt_tr", 4 * e + f + 1)
                after(act, "up_done", STEPS * (e - 1))
                hi_of(xT[i][0][:, kt, g * HALF:(g + 1) * HALF], x_ps[:], "e_xt_hi")

            split_weights(0, 0, 0)
            split_weights(0, 0, 1)
            for f in range(2):
                xt_high(0, 0, f)

            def body(e, i, more):
                after(act, "b1_ready", e + 2)
                for t in range(STEPS):
                    k = e * STEPS + t
                    if more and t >= 12:
                        xt_high(e + 1, 1 - i, t - 12)
                    if isinstance(e, int) and e == 0 and t in (3, 4):
                        xt_high(0, 0, t - 1)
                    bias = b1_e[i][:, t % DT:t % DT + 1]
                    after(act, "up_done", k + 1)
                    after(act, "h_lo", k - 1)
                    nc.scalar.activation(hid[:, t % 2, :], up_ps[t % 2][:], ACT.Gelu, bias=bias)
                    after(act, "down_done", k - (RING - 1))
                    nc.scalar.activation(hT[0][:, t % RING, :], up_ps[t % 2][:], ACT.Gelu,
                                         bias=bias).then_inc(s["h_hi"], 1)
                    if more:
                        if t in (5, 7):
                            split_weights(e + 1, 1 - i, (t - 5) // 2)
            experts(act, body)

        @block.tensor
        def _(pe):
            PARTS = [(0, 0), (0, 1), (1, 0)]

            pe.wait_ge(s["c_in"], 32)
            nc.tensor.transpose(l_ps[:, 0:E * DT], b1_rows[:], ident[0:E * DT, 0:E * DT])\
                .then_inc(s["b1_tr"], 1)
            pe.wait_ge(s["b1_ready"], 1)
            def turn_halves(out, in_):
                for g in range(EH):
                    last = nc.tensor.transpose(out[:, g * P:(g + 1) * P], in_[:, g, :], ident[:])
                last.then_inc(s["turned"], 1)

            def total(which, out):
                return nc.tensor.matmul(out, groups[:, which, :],
                                        count_bf[:].rearrange("p k g -> p (k g)")
                                        [:, 0:out.shape[1]], start=True, stop=True)

            turn_halves(x_ps, score[:].rearrange("p (g e) b -> p g (e b)", g=EH))
            with pe.Fori(0, ITERATIONS) as r:
                pe.wait_ge(s["counted"], r + 1)
                total(0, l_ps[:, 0:3 * EH]).then_inc(s["totalled"], 1)
            pe.wait_ge(s["counted"], ITERATIONS + 1)
            total(0, l_ps[:, 0:EH]).then_inc(s["totalled"], 1)
            for k in range(2):
                pe.wait_ge(s["marked"], k + 1)
                total(1, l_ps[:, 0:EH]).then_inc(s["ranked"], 1)
            pe.wait_ge(s["marked"], 3)
            turn_halves(x_ps, rank)

            def write_list(e):
                after(pe, "hot_ready", e + 1)
                after(pe, "tok_ready", e)
                for t in range(NB):
                    last = nc.tensor.matmul(l_ps[0:LIST_A, 0:2 * LIST_A], hot_a[:, t, :],
                                            hot_b[:, t, 1:3, :].rearrange("p k b -> p (k b)"),
                                            start=t == 0, stop=t == NB - 1)
                last.then_inc(s["listed"], 1)

            def turn(e, i, f):
                g, kt = divmod(f, 2)
                after(pe, f"rows_in{g}", 16 * TB * (e + 1))
                after(pe, "e_xt_lo", 4 * e + f)
                for c in range(TB):
                    last = nc.tensor.transpose(x_ps[:, c * P:(c + 1) * P],
                                               got[i][:, TB * g + c, kt * P:(kt + 1) * P], ident[:])
                last.then_inc(s["e_xt_tr"], 1)

            def up(e, i, t):
                k = e * STEPS + t
                half, dt = divmod(t, DT)
                after(pe, "h_hi", k - 1)
                todo = [(w1[i][x][:, kt, dt * P:(dt + 1) * P],
                         xT[i][z][:, kt, half * HALF:(half + 1) * HALF])
                        for kt in range(KT) for x, z in PARTS]
                for c, (l, r) in enumerate(todo):
                    last = nc.tensor.matmul(up_ps[t % 2][:], l, r, start=c == 0,
                                            stop=c == len(todo) - 1)
                last.then_inc(s["up_done"], 1)

            def down(e, i, t):
                k = e * STEPS + t
                half, dt = divmod(t, DT)
                if dt == 0:
                    after(pe, "y_b2", e * 4 + 2 * half - 2)
                after(pe, "h_lo", k + 1)
                for c in range(TB):
                    for n, (x, z) in enumerate(PARTS):
                        last = nc.tensor.matmul(
                            y_ps[half][c // 2][:, (c % 2) * M:(c % 2 + 1) * M],
                            hT[x][:, t % RING, c * P:(c + 1) * P], w2[i][z][:, dt, :],
                            start=dt == 0 and c % 2 == 0 and n == 0,
                            stop=dt == DT - 1 and c % 2 == 1 and n == 2)
                last.then_inc(s["down_done"], 1)

            write_list(0)
            for f in range(2):
                turn(0, 0, f)

            def body(e, i, more):
                for t in range(STEPS):
                    if t == 0:
                        after(pe, "e_xt_lo", 4 * e + 2)
                        after(pe, "w_lo2", 2 * e + 2)
                    if t == DT:
                        after(pe, "e_xt_lo", 4 * e + 4)
                    up(e, i, t)
                    if t >= LAG:
                        down(e, i, t - LAG)
                    elif not (isinstance(e, int) and e == 0):
                        down(e - 1, 1 - i, STEPS + t - LAG)
                    if more and t == 2:
                        write_list(e + 1)
                    if more and 11 <= t < 15:
                        turn(e + 1, 1 - i, t - 11)
                    if isinstance(e, int) and e == 0 and t in (2, 3):
                        turn(0, 0, t)
            experts(pe, body)
            for t in range(LAG):
                down(E - 1, 1, STEPS + t - LAG)


def build(nc, a):
    with (nc.sbuf_tensor("score", [P, E, NB], F32) as score,
          nc.sbuf_tensor("ident", [P, P], F32) as ident):
        with nc.sbuf_tensor("h2", [P, NB, M], F32) as h2:
            build_attention(nc, a, ident, h2)
            build_router(nc, a, ident, h2, score)
        build_experts(nc, a, ident, score)


def kernel(x, L0_tok_weight, L0_attn_w_aq, L0_attn_w_ak, L0_attn_w_av, L0_attn_w_ao,
           L0_ffn_Wr, L0_ffn_W1, L0_ffn_b1, L0_ffn_W2, L0_ffn_b2):
    import numpy as np
    import concourse.bacc as bacc
    from concourse.bass_utils import run_bass_kernel_spmd

    half = D // 2
    freqs = np.power(np.float32(10000.0), -np.arange(half, dtype=np.float32) / np.float32(half))
    angles = np.arange(T, dtype=np.float32)[None, :] * freqs[:, None].astype(np.float32)
    cos, sin = np.cos(angles), np.sin(angles)
    rope = np.stack([np.concatenate([cos, cos]), np.concatenate([-sin, sin])], 1)
    i = np.arange(P)
    later = i[None, :] > i[:, None]
    same = i[None, :] // NB == i[:, None] // NB

    arrays = {
        "ids": np.ascontiguousarray(x.reshape(B, TB, P).transpose(0, 2, 1)),
        "emb": L0_tok_weight,
        "wq": L0_attn_w_aq.reshape(M, H * D), "wk": L0_attn_w_ak.reshape(M, H * D),
        "wv": L0_attn_w_av.reshape(M, H * D), "wo": L0_attn_w_ao,
        "wr": L0_ffn_Wr, "w1": L0_ffn_W1, "b1": L0_ffn_b1, "w2": L0_ffn_W2, "b2": L0_ffn_b2,
        "rope": rope.astype(np.float32), "ident": np.eye(P, dtype=np.float32),
        "mask": np.where(later, np.float32(1e30), np.float32(0)),
        "groups": np.stack([same, same & later], 1).astype(np.float32),
    }
    arrays = {k: np.ascontiguousarray(v) for k, v in arrays.items()}
    nc = bacc.Bacc("TRN2", target_bir_lowering=False, num_devices=1)
    a = {k: nc.dram_tensor(f"in_{k}", v.shape, mybir.dt.from_np(v.dtype), kind="ExternalInput").ap()
         for k, v in arrays.items()}
    a["out"] = nc.dram_tensor("out_0", (N, M), F32, kind="ExternalOutput").ap()
    a["rows"] = nc.dram_tensor("routed_rows", (N, ROW), F32, kind="Internal").ap()
    build(nc, a)
    r = run_bass_kernel_spmd(nc, [{f"in_{k}": v for k, v in arrays.items()}], core_ids=[0])
    return r.results[0]["out_0"].reshape(B, T, M)
```

```python
import concourse.bass as bass
from concourse import mybir
from concourse.alu_op_type import AluOpType as ALU
from contextlib import ExitStack

F32 = mybir.dt.float32
F32R = mybir.dt.float32r
BF16 = mybir.dt.bfloat16
I32 = mybir.dt.int32
ACT = mybir.ActivationFunctionType
AX = mybir.AxisListType

P = 128
B, T, M = 8, 512, 256
H, D = 8, 128
VOCAB = 8000
N = B * T
TB = T // P
KT = M // P
NB = N // P
E, DI, TOPK = 8, 1024, 1024
EPS = 1e-5

ROWS = [(3, 0, 0, 0), (2, 1, 0, 512), (0, 1, 384, 896), (1, 0, 0, 1024)]
P_COL = {ib: col for ib, _, _, col in ROWS}
ROW_AT = {ib: k for k, (ib, _, _, _) in enumerate(ROWS)}
P_COLS = sum((ib + 1) * P for ib in range(TB))
PT_COL = {0: 0, 1: 512, 2: 896, 3: 1152}
T_FILLS = [([(2, 2), (2, 3), (3, 3)], 896), ([(0, 0), (0, 1), (0, 2), (0, 3)], 0),
           ([(1, 1), (1, 2), (1, 3)], 512)]
V_SLOT = {0: [0, 1], 1: [2], 2: [3], 3: [4], 4: [5], 5: [6], 6: [7], 7: []}


def build_attention(nc, a, ident, h2, x2, wr, shared):
    ctx = ExitStack()
    with ctx:
        def sb(name, shape, dt=F32):
            return ctx.enter_context(nc.sbuf_tensor(name, shape, dt))

        def sem(name):
            return ctx.enter_context(nc.semaphore(name))

        w_qkv = {k: [sb(f"w{k}_{p}", [P, KT, H * D], F32R) for p in ("hi", "lo")] for k in "qkv"}
        w_o = [sb(f"wo_{p}", [P, H, M], F32R) for p in ("hi", "lo")]
        rope_k = sb("rope_k", [P, 2, T])
        rope_q = sb("rope_q", [P, 2, T])
        ident_bf = sb("ident_bf", [P, P], BF16)
        mask_bf = sb("mask_bf", [P, P], BF16)
        neg_half = sb("neg_half", [P, TB])
        ids = sb("ids", [P, TB], I32)
        emb = sb("emb", [P, TB, M])
        emb_res = sb("emb_res", [P, TB, M])
        xn = h2
        stats = sb("stats", [P, TB, 6])
        mean_var = sb("mean_var", [P, TB, 2])
        rstd = sb("rstd", [P, TB])
        stats2 = sb("stats2", [P, TB, 6])
        mean_var2 = sb("mean_var2", [P, TB, 2])
        rstd2 = sb("rstd2", [P, TB])
        xT = [sb(f"xT_{p}", [P, KT, T], F32R) for p in ("hi", "lo")]
        q_cos, q_sin = sb("q_cos", [P, T]), sb("q_sin", [P, T])
        k_cos, k_sin = sb("k_cos", [P, T]), sb("k_sin", [P, T])
        qT = [sb(f"qT_{p}", [P, 2, T], F32R) for p in ("hi", "lo")]
        kT = [sb(f"kT_{p}", [P, 2, T], F32R) for p in ("hi", "lo")]
        v = [sb(f"v_{p}", [P, 2 * TB, 4 * D], F32R) for p in ("hi", "lo")]
        prob = sb("prob", [P, 2, P_COLS])
        mask_f = prob[:, 0, 0:P]
        row_min = sb("row_min", [P, 2, TB])
        row_sum = sb("row_sum", [P, 2, TB])
        row_inv = sb("row_inv", [P, 2, TB])
        pT = [sb(f"pT_{p}", [P, P_COLS], F32R) for p in ("hi", "lo")]
        oT = [sb(f"oT_{p}", [P, T], F32R) for p in ("hi", "lo")]

        bank = [ctx.enter_context(nc.psum_tensor(f"bank{i}", [P, 512], F32)) for i in range(8)]
        proj_ps, s_ps, r_ps = bank[0:2], bank[2:4], bank[6:8]
        o_ps, t_ps = bank[4], [bank[5], bank[4], bank[5]]

        names = """wq_in wk_in wv_in wo_in tables_in w_hi w_lo consts
            ids_in emb_in res_in stats_done aggr_done var_eps rstd_done xn_ready xt_tr xt_hi xt_lo
            q_proj k_proj v_proj q_rope k_rope q_add k_add q_hi k_hi q_lo k_lo v_hi v_lo
            s_done s_min exp_done inv_done norm_done t_done t_hi t_lo o_done o_hi o_lo
            out_done r_evac 
            stats2_done aggr2_done var2_eps rstd2_done apart""".split()
        s = {n: sem(n) for n in names} | shared

        block = ctx.enter_context(nc.Block())

        def after(eng, name, count):
            if isinstance(count, int) and count <= 0:
                return
            eng.wait_ge(s[name], count)

        def alone(eng):
            eng.sem_inc(s["apart"], 1)

        def batches(eng, body):
            body(0, range(8), lambda h: h >= 0)
            with eng.Fori(1, B - 1) as b:
                body(b, range(8), lambda h: True)
            body(B - 1, range(11), lambda h: h < H)

        wsrc = {k: a[f"w{k}"].rearrange("(t p) n -> p t n", p=P) for k in "qkv"}
        wraw = {k: x2[:, 8 * i:8 * i + 8, :].rearrange("p (t g) m -> p t (g m)", t=KT)
                for i, k in enumerate("qkv")}
        wraw_o = x2[:, 24:32, :]
        out_b = a["out"].rearrange("(b p) m -> p b m", p=P)
        rows_b = a["rows"].rearrange("(b p) m -> p b m", p=P)

        @block.sync
        def _(sp):
            sp.dma_start(ids[:], a["ids"][0]).then_inc(s["ids_in"], 16)
            sp.dma_start(ident[:], a["ident"][:, :]).then_inc(s["tables_in"], 16)
            sp.dma_start(mask_f, a["mask"][:, :]).then_inc(s["tables_in"], 16)
            sp.dma_start(rope_k[:], a["rope"][:, :, :]).then_inc(s["tables_in"], 16)
            for k in "qkv":
                if k == "v":
                    sp.wait_ge(s["emb_in"], 16 * TB)
                sp.dma_start(wraw[k], wsrc[k]).then_inc(s[f"w{k}_in"], 16)
            sp.dma_start(wraw_o, a["wo"].rearrange("h d m -> d h m")).then_inc(s["wo_in"], 16)

            sp.dma_start(wr[:], a["wr"].rearrange("(t p) e -> p t e", p=P))\
                .then_inc(s["wr_in"], 16)

            def store_h2(b):
                after(sp, "r_evac", b + 1)
                sp.dma_start(out_b[:, bass.ds(b * TB, TB), :], h2[:]).then_inc(s["h2_out"], 16)

            def store_x2(b):
                after(sp, "x2_ready", TB * (b + 1))
                sp.dma_start(rows_b[:, bass.ds(b * TB, TB), 0:M], x2[:, bass.ds(b * TB, TB), :])\
                    .then_inc(s["x2_out"], 16)

            def body(b, slots, ok):
                if not (isinstance(b, int) and b == 0):
                    store_h2(b - 1)
                after(sp, "r_evac", b)
                after(sp, "emb_in", (b + 1) * 16 * TB)
                sp.dma_start(emb_res[:], emb[:]).then_inc(s["res_in"], 16)
                if len(slots) == H:
                    sp.dma_start(ids[:], a["ids"][b + 1]).then_inc(s["ids_in"], 16)
                if not (isinstance(b, int) and b == 0):
                    store_x2(b - 1)
            batches(sp, body)
            store_h2(B - 1)

        @block.gpsimd
        def _(pool):
            nc.gpsimd.memset(neg_half[:], -0.5).then_inc(s["consts"], 1)

            def gather(b, blocks):
                after(pool, "ids_in", (b + 1) * 16)
                after(pool, "res_in", b * 16)
                after(pool, "xn_ready", b)
                alone(pool)
                for tb in blocks:
                    pool.indirect_dma_start(emb[:, tb, :], None, a["emb"][:, :],
                                            bass.IndirectOffsetOnAxis(ids[:, tb:tb + 1], 0))\
                        .then_inc(s["emb_in"], 16)

            def rsqrt(b):
                after(pool, "aggr_done", b + 1)
                alone(pool)
                nc.gpsimd.tensor_scalar(rstd[:], mean_var[:, :, 1], EPS, None, ALU.add)\
                    .then_inc(s["var_eps"], 1)
                after(pool, "var_eps", b + 1)
                nc.gpsimd.tensor_tensor(rstd[:], rstd[:], neg_half[:], ALU.pow)\
                    .then_inc(s["rstd_done"], 1)

            def rsqrt2(b):
                after(pool, "aggr2_done", b + 1)
                alone(pool)
                nc.gpsimd.tensor_scalar(rstd2[:], mean_var2[:, :, 1], EPS, None, ALU.add)\
                    .then_inc(s["var2_eps"], 1)
                after(pool, "var2_eps", b + 1)
                nc.gpsimd.tensor_tensor(rstd2[:], rstd2[:], neg_half[:], ALU.pow)\
                    .then_inc(s["rstd2_done"], 1)

            def norm(b, h, ks):
                alone(pool)
                for k in ks:
                    ib, _, _, col = ROWS[k]
                    pr = prob[:, h % 2, col:col + (ib + 1) * P]
                    nc.gpsimd.tensor_scalar(pr, pr, row_inv[:, h % 2, k:k + 1], 1.0,
                                            ALU.mult, ALU.mult).then_inc(s["norm_done"], 1)

            def add(b, h, x):
                n = b * H + h
                cos, sin = (q_cos, q_sin) if x == "q" else (k_cos, k_sin)
                after(pool, f"{x}_rope", n + 1)
                nc.gpsimd.tensor_tensor(cos[:], cos[:], sin[:], ALU.add).then_inc(s[f"{x}_add"], 1)

            def low(b, h, x):
                n = b * H + h
                cos, out = (q_cos, qT) if x == "q" else (k_cos, kT)
                after(pool, f"{x}_hi", n + 1)
                nc.gpsimd.tensor_tensor(out[1][:, h % 2, :], cos[:], out[0][:, h % 2, :].bitcast(F32),
                                        ALU.subtract).then_inc(s[f"{x}_lo"], 1)

            pool.wait_ge(s["consts"], 1)
            gather(0, range(TB))
            rsqrt(0)

            def body(b, slots, ok):
                for h in slots:
                    n = b * H + h
                    live = ok(h) and h < H
                    if live:
                        add(b, h, "q")
                    if ok(h - 2):
                        after(pool, "inv_done", 2 * (n - 2) + 2)
                        norm(b, h - 2, [3])
                    if live:
                        low(b, h, "q")
                        add(b, h, "k")
                        low(b, h, "k")
                    if len(slots) == H and h in (3, 4, 5):
                        gather(b + 1, [h - 3])
                    if len(slots) == H and h == 6:
                        rsqrt(b + 1)
                    if ok(h - 1):
                        after(pool, "inv_done", 2 * (n - 1) + 1)
                        norm(b, h - 1, [0, 1, 2])
                    if len(slots) == H and h == 5:
                        gather(b + 1, [3])
                    if h == 4 and not (isinstance(b, int) and b == 0):
                        rsqrt2(b - 1)
            batches(pool, body)

        @block.scalar
        def _(act):
            def hi_of(out, in_, name):
                nc.scalar.activation(out, in_, ACT.Copy).then_inc(s[name], 1)

            act.wait_ge(s["tables_in"], 48)
            nc.scalar.activation(ident_bf[:], ident[:], ACT.Copy).then_inc(s["w_hi"], 1)
            nc.scalar.activation(mask_bf[:], mask_f, ACT.Copy).then_inc(s["w_hi"], 1)
            nc.scalar.activation(rope_q[:], rope_k[:], ACT.Copy, scale=-1.0 / D)\
                .then_inc(s["w_hi"], 1)

            def xt(b):
                for kt in range(KT):
                    after(act, "xt_tr", KT * b + kt + 1)
                    hi_of(xT[0][:, kt, :], proj_ps[kt][:], "xt_hi")

            def exp(b, h, k):
                n = b * H + h
                ib, bk, pc, col = ROWS[k]
                w = (ib + 1) * P
                after(act, "s_min", TB * n + (1, 3, 3, 4)[k])
                after(act, "t_done", 3 * (n - 2) + 3)
                nc.scalar.activation(prob[:, h % 2, col:col + w], s_ps[bk][:, pc:pc + w], ACT.Exp,
                                     bias=row_min[:, h % 2, k:k + 1], scale=-1.0,
                                     accum_out=row_sum[:, h % 2, k:k + 1]).then_inc(s["exp_done"], 1)

            def t_high(b, h, f):
                n = b * H + h
                pairs, col = T_FILLS[f]
                w = len(pairs) * P
                after(act, "t_done", 3 * n + f + 1)
                after(act, "o_done", n)
                hi_of(pT[0][:, col:col + w], t_ps[f][:, 0:w], "t_hi")

            def qk_high(b, h, x):
                n = b * H + h
                cos, out = (q_cos, qT) if x == "q" else (k_cos, kT)
                after(act, f"{x}_add", n + 1)
                after(act, "s_done", 3 * (n - 2) + 3)
                hi_of(out[0][:, h % 2, :], cos[:], f"{x}_hi")

            def v_high(b, h, i):
                t = V_SLOT[h][i]
                after(act, "v_proj", 2 * TB * b + t + 1)
                after(act, "o_done", (b - 1) * H + 4 * (t // TB) + 4)
                hi_of(v[0][:, t, :], proj_ps[i][:], "v_hi")

            for k in "qk":
                act.wait_ge(s[f"w{k}_in"], 16)
                hi_of(w_qkv[k][0][:], wraw[k], "w_hi")
            xt(0)
            act.wait_ge(s["wv_in"], 16)
            hi_of(w_qkv["v"][0][:], wraw["v"], "w_hi")
            act.wait_ge(s["wo_in"], 16)
            hi_of(w_o[0][:], wraw_o, "w_hi")

            def body(b, slots, ok):
                for h in slots:
                    n = b * H + h
                    live = ok(h) and h < H
                    if ok(h - 3):
                        after(act, "o_done", n - 3 + 1)
                        after(act, "out_done", n - 3)
                        hi_of(oT[0][:], o_ps[:], "o_hi")
                    if live:
                        qk_high(b, h, "q")
                    if ok(h - 2):
                        t_high(b, h - 2, 0)
                    if ok(h - 1):
                        exp(b, h - 1, 0)
                    if live:
                        for i in range(len(V_SLOT[h])):
                            v_high(b, h, i)
                    if len(slots) == H and h == 7:
                        xt(b + 1)
                    if live:
                        qk_high(b, h, "k")
                    if ok(h - 1):
                        exp(b, h - 1, 1)
                    if ok(h - 2):
                        t_high(b, h - 2, 1)
                    if ok(h - 1):
                        exp(b, h - 1, 2)
                    if ok(h - 2):
                        t_high(b, h - 2, 2)
                    if ok(h - 1):
                        exp(b, h - 1, 3)
            batches(act, body)

        @block.vector
        def _(dve):
            def low_of(out, in_, hi, name):
                nc.vector.tensor_tensor(out, in_, hi.bitcast(F32), ALU.subtract)\
                    .then_inc(s[name], 1)

            def stats_of(b, blocks):
                after(dve, "emb_in", (b + 1) * 16 * TB)
                for tb in blocks:
                    nc.vector.bn_stats(stats[:, tb, :], emb[:, tb, :]).then_inc(s["stats_done"], 1)

            def aggregate(b):
                after(dve, "stats_done", TB * (b + 1))
                alone(dve)
                for tb in range(TB):
                    last = nc.vector.bn_aggr(mean_var[:, tb, :], stats[:, tb, :])
                last.then_inc(s["aggr_done"], 1)

            def normalise(b):
                after(dve, "rstd_done", b + 1)
                after(dve, "h2_out", 16 * (b - 1))
                after(dve, "xt_tr", KT * b)
                for tb in range(TB):
                    last = nc.vector.tensor_scalar(xn[:, tb, :], emb[:, tb, :], mean_var[:, tb, 0:1],
                                                   rstd[:, tb:tb + 1], ALU.subtract, ALU.mult)
                last.then_inc(s["xn_ready"], 1)

            def xt(b):
                for kt in range(KT):
                    after(dve, "xt_hi", KT * b + kt + 1)
                    low_of(xT[1][:, kt, :], proj_ps[kt][:], xT[0][:, kt, :], "xt_lo")

            def rope(b, h, x):
                n = b * H + h
                ps, table, cos, sin = ((proj_ps[0], rope_q, q_cos, q_sin) if x == "q" else
                                       (proj_ps[1], rope_k, k_cos, k_sin))
                after(dve, f"{x}_proj", n + 1)
                after(dve, f"{x}_lo", n)
                nc.vector.tensor_tensor(cos[:], ps[:], table[:, 0, :], ALU.mult)
                nc.vector.tensor_tensor(sin[0:64, :], ps[64:128, :], table[0:64, 1, :], ALU.mult)
                nc.vector.tensor_tensor(sin[64:128, :], ps[0:64, :], table[64:128, 1, :], ALU.mult)\
                    .then_inc(s[f"{x}_rope"], 1)

            def t_low(b, h, f):
                n = b * H + h
                pairs, col = T_FILLS[f]
                w = len(pairs) * P
                after(dve, "t_hi", 3 * n + f + 1)
                low_of(pT[1][:, col:col + w], t_ps[f][:, 0:w], pT[0][:, col:col + w], "t_lo")

            def minimum(b, h, k):
                n = b * H + h
                ib, bk, pc, _ = ROWS[k]
                nc.vector.tensor_reduce(row_min[:, h % 2, k:k + 1], s_ps[bk][:, pc:pc + (ib + 1) * P],
                                        AX.X, ALU.min).then_inc(s["s_min"], 1)

            def inverse(b, h, lo, hi):
                nc.vector.reciprocal(row_inv[:, h % 2, lo:hi], row_sum[:, h % 2, lo:hi])\
                    .then_inc(s["inv_done"], 1)

            def evacuate(b):
                after(dve, "out_done", H * (b + 1))
                after(dve, "res_in", 16 * (b + 1))
                after(dve, "xt_tr", KT * (b + 2) if not isinstance(b, int) or b < B - 1 else KT * B)
                for i in range(2):
                    last = nc.vector.tensor_tensor(
                        h2[:, 2 * i:2 * i + 2, :],
                        r_ps[i][:].rearrange("p (t m) -> p t m", m=M),
                        emb_res[:, 2 * i:2 * i + 2, :], ALU.add)
                last.then_inc(s["r_evac"], 1)

            def stats2_of(b, blocks):
                after(dve, "r_evac", b + 1)
                for tb in blocks:
                    last = nc.vector.bn_stats(stats2[:, tb, :], h2[:, tb, :])
                last.then_inc(s["stats2_done"], 1)

            def aggregate2(b):
                after(dve, "stats2_done", 2 * b + 2)
                alone(dve)
                for tb in range(TB):
                    last = nc.vector.bn_aggr(mean_var2[:, tb, :], stats2[:, tb, :])
                last.then_inc(s["aggr2_done"], 1)

            def normalise2(b, blocks):
                after(dve, "rstd2_done", b + 1)
                if isinstance(b, int) and b == 0:
                    dve.wait_ge(s["w_lo"], 4)
                for tb in blocks:
                    nc.vector.tensor_scalar(
                        x2[:, bass.ds(b * TB + tb, 1), :].rearrange("p o m -> p (o m)"),
                        h2[:, tb, :], mean_var2[:, tb, 0:1], rstd2[:, tb:tb + 1],
                        ALU.subtract, ALU.mult).then_inc(s["x2_ready"], 1)

            def layernorm2(b, h, half):
                if isinstance(b, int) and b == 0 or h >= H:
                    return
                if h == 3:
                    stats2_of(b - 1, range(2 * half, 2 * half + 2))
                if h == 5:
                    normalise2(b - 1, range(2 * half, 2 * half + 2))

            after(dve, "w_hi", 4)
            low_of(w_qkv["q"][1][:], wraw["q"], w_qkv["q"][0][:], "w_lo")
            stats_of(0, range(TB))
            aggregate(0)
            after(dve, "w_hi", 5)
            low_of(w_qkv["k"][1][:], wraw["k"], w_qkv["k"][0][:], "w_lo")
            normalise(0)
            xt(0)
            after(dve, "w_hi", 6)
            low_of(w_qkv["v"][1][:], wraw["v"], w_qkv["v"][0][:], "w_lo")

            def body(b, slots, ok):
                for h in slots:
                    n = b * H + h
                    live = ok(h) and h < H
                    if live:
                        rope(b, h, "q")
                    if ok(h - 2):
                        after(dve, "exp_done", TB * (n - 2) + 4)
                        inverse(b, h - 2, 3, 4)
                    if live:
                        rope(b, h, "k")
                    if isinstance(b, int) and b == 0 and h == 0:
                        after(dve, "w_hi", 7)
                        low_of(w_o[1][:], wraw_o, w_o[0][:], "w_lo")
                    if ok(h - 3):
                        after(dve, "o_hi", n - 3 + 1)
                        low_of(oT[1][:], o_ps[:], oT[0][:], "o_lo")
                    if ok(h - 2):
                        t_low(b, h - 2, 0)
                    if ok(h - 1):
                        after(dve, "s_done", 3 * (n - 1) + 1)
                        minimum(b, h - 1, 0)
                        after(dve, "s_done", 3 * (n - 1) + 2)
                        minimum(b, h - 1, 1)
                        minimum(b, h - 1, 2)
                    layernorm2(b, h, 0)
                    if len(slots) == H and h == 6:
                        stats_of(b + 1, [0, 1])
                    if live:
                        for i, t in enumerate(V_SLOT[h]):
                            after(dve, "v_hi", 2 * TB * b + t + 1)
                            low_of(v[1][:, t, :], proj_ps[i][:], v[0][:, t, :], "v_lo")
                    if len(slots) == H and h == 7:
                        xt(b + 1)
                    layernorm2(b, h, 1)
                    if len(slots) == H and h == 6:
                        stats_of(b + 1, [2, 3])
                        aggregate(b + 1)
                    if ok(h - 2):
                        t_low(b, h - 2, 1)
                    if ok(h - 1):
                        after(dve, "s_done", 3 * (n - 1) + 3)
                        minimum(b, h - 1, 3)
                    if ok(h - 2):
                        t_low(b, h - 2, 2)
                    if ok(h - 1):
                        after(dve, "exp_done", TB * (n - 1) + 3)
                        inverse(b, h - 1, 0, 3)
                    if h == 2 and ok(h - 3):
                        evacuate(b - 1)
                    if h == 3 and not (isinstance(b, int) and b == 0):
                        aggregate2(b - 1)
                    if h == 10:
                        evacuate(b)
                    if len(slots) == H and h == 6:
                        normalise(b + 1)
            batches(dve, body)

        @block.tensor
        def _(pe):
            PARTS = [(0, 0), (0, 1), (1, 0)]

            def products(out, pairs, start=True, stop=True):
                todo = [(l[i], r[j]) for l, r in pairs for i, j in PARTS]
                for c, (l, r) in enumerate(todo):
                    last = nc.tensor.matmul(out, l, r, start=start and c == 0,
                                            stop=stop and c == len(todo) - 1)
                return last

            def xt(b):
                after(pe, "xn_ready", b + 1)
                for kt in range(KT):
                    after(pe, "k_rope" if kt else "q_rope", b * H)
                    for tb in range(TB):
                        last = nc.tensor.transpose(proj_ps[kt][:, tb * P:(tb + 1) * P],
                                                   xn[:, tb, kt * P:(kt + 1) * P], ident[:])
                    last.then_inc(s["xt_tr"], 1)

            def project(b, h, x):
                n = b * H + h
                ps = proj_ps[0 if x == "q" else 1]
                if h == 0:
                    after(pe, "xt_lo", KT * (b + 1))
                elif x == "q":
                    after(pe, "v_lo", 2 * TB * b + V_SLOT[h - 1][-1] + 1)
                elif h == 1:
                    after(pe, "v_lo", 2 * TB * b + 2)
                else:
                    after(pe, "k_rope", n)
                products(ps[:], [([w[:, kt, h * D:(h + 1) * D] for w in w_qkv[x]],
                                  [t[:, kt, :] for t in xT]) for kt in range(KT)])\
                    .then_inc(s[f"{x}_proj"], 1)

            def values(b, h, i):
                n = b * H + h
                g, jb = divmod(V_SLOT[h][i], TB)
                after(pe, "k_rope" if i else "q_rope", n + 1)
                products(proj_ps[i][:], [([t[:, kt, jb * P:(jb + 1) * P] for t in xT],
                                          [w[:, kt, g * 512:(g + 1) * 512] for w in w_qkv["v"]])
                                         for kt in range(KT)]).then_inc(s["v_proj"], 1)

            def scores(b, h, ks):
                n = b * H + h
                for k in ks:
                    ib, bk, pc, _ = ROWS[k]
                    w = (ib + 1) * P
                    products(s_ps[bk][:, pc:pc + w],
                             [([q[:, h % 2, ib * P:(ib + 1) * P] for q in qT],
                               [x[:, h % 2, 0:w] for x in kT])], stop=False)
                    last = nc.tensor.matmul(s_ps[bk][:, pc + ib * P:pc + w], ident_bf[:], mask_bf[:],
                                            start=False, stop=True)
                last.then_inc(s["s_done"], 1)

            def turn(b, h, f):
                n = b * H + h
                after(pe, "o_lo" if f == 1 else "t_lo", n if f == 1 else 3 * n + f // 2)
                for c, (jb, ib) in enumerate(T_FILLS[f][0]):
                    col = P_COL[ib] + jb * P
                    last = nc.tensor.transpose(t_ps[f][:, c * P:(c + 1) * P],
                                               prob[:, h % 2, col:col + P], ident[:])
                last.then_inc(s["t_done"], 1)

            def weigh(b, h):
                n = b * H + h
                g = (h % H) // 4
                after(pe, "t_lo", 3 * n + 2)
                after(pe, "v_lo", 2 * TB * b + TB * (g + 1) if 0 <= h < H
                      else 2 * TB * (b - 1) + TB * (g + 1))
                order = [0, 2, 3, 1]
                for jb in order:
                    if jb == order[-1]:
                        after(pe, "t_lo", 3 * n + 3)
                    w = T - jb * P
                    c = (h % 4) * D
                    last = products(o_ps[:, jb * P:T],
                                    [([x[:, g * TB + jb, c:c + D] for x in v],
                                      [x[:, PT_COL[jb]:PT_COL[jb] + w] for x in pT])],
                                    start=jb == 0, stop=jb == order[-1])
                last.then_inc(s["o_done"], 1)

            def output(b, h, half):
                n = b * H + h
                hh = h % H
                after(pe, "o_lo", n + 1)
                if isinstance(b, int) and b == 0 and h == 0:
                    pe.wait_ge(s["w_lo"], 4)
                if hh == 0:
                    after(pe, "r_evac", b if h >= 0 else b - 1)
                for ib in (2 * half, 2 * half + 1):
                    last = products(r_ps[half][:, (ib % 2) * M:(ib % 2 + 1) * M],
                                    [([x[:, ib * P:(ib + 1) * P] for x in oT],
                                      [w[:, hh, :] for w in w_o])],
                                    start=hh == 0 and ib % 2 == 0,
                                    stop=hh == H - 1 and ib % 2 == 1)
                if half:
                    last.then_inc(s["out_done"], 1)

            pe.wait_ge(s["tables_in"], 48)
            xt(0)

            def body(b, slots, ok):
                for h in slots:
                    n = b * H + h
                    live = ok(h) and h < H
                    if live:
                        if isinstance(b, int) and b == 0 and h == 0:
                            pe.wait_ge(s["w_lo"], 1)
                        project(b, h, "q")
                        if isinstance(b, int) and b == 0 and h == 0:
                            pe.wait_ge(s["w_lo"], 2)
                        project(b, h, "k")
                    if ok(h - 3):
                        weigh(b, h - 3)
                    if ok(h - 2):
                        after(pe, "norm_done", TB * (n - 2) + 2)
                        turn(b, h - 2, 0)
                    if ok(h - 1):
                        after(pe, "q_lo", n)
                        after(pe, "k_lo", n)
                        after(pe, "exp_done", TB * (n - 1))
                        scores(b, h - 1, [0])
                        after(pe, "exp_done", TB * (n - 2) + 3)
                        scores(b, h - 1, [1, 2])
                    if live:
                        if isinstance(b, int) and b == 0 and h == 0:
                            pe.wait_ge(s["w_lo"], 3)
                        for i in range(len(V_SLOT[h])):
                            values(b, h, i)
                    if len(slots) == H and h == 7:
                        xt(b + 1)
                    if ok(h - 3):
                        output(b, h - 3, 0)
                    if ok(h - 2):
                        after(pe, "norm_done", TB * (n - 2) + 4)
                        turn(b, h - 2, 1)
                    if ok(h - 3):
                        output(b, h - 3, 1)
                    if ok(h - 1):
                        after(pe, "exp_done", TB * (n - 1) + 1)
                        scores(b, h - 1, [3])
                    if ok(h - 2):
                        turn(b, h - 2, 2)
            batches(pe, body)
LIST_A = 32
CH = TOPK // P
HALF = 512
DT = DI // P
ROW = M + E


def build_router(nc, a, ident, h2, x2, wr, score, score_rows, shared):
    ctx = ExitStack()
    with ctx:
        def sb(name, shape, dt=F32):
            return ctx.enter_context(nc.sbuf_tensor(name, shape, dt))

        NG = NB // TB
        xT = sb("r_xT", [P, 2, KT, TB * P])
        lT = sb("r_lT", [E, 2, TB * P])
        top = sb("r_top", [P, NB])
        total = sb("r_total", [P, NB])
        logit = sb("r_logit", [P, NB, E])
        stats, mean_var = sb("r_stats", [P, TB, 6]), sb("r_mean_var", [P, TB, 2])
        rstd, neg_half = sb("r_rstd", [P, TB]), sb("r_neg_half", [P, TB])
        x_ps = [[ctx.enter_context(nc.psum_tensor(f"rx{i}{kt}", [P, TB * P], F32))
                 for kt in range(KT)] for i in range(2)]
        lT_ps = [ctx.enter_context(nc.psum_tensor(f"r_lT_ps{i}", [E, TB * P], F32))
                 for i in range(2)]
        l_ps = ctx.enter_context(nc.psum_tensor("r_logits", [P, NB, E], F32))
        names = "r_tr r_copy0 r_copy1 r_logitsT r_lT r_logits_done r_step r_exp r_score r_const r_aggr r_eps r_rstd".split()
        s = {n: ctx.enter_context(nc.semaphore(n)) for n in names} | shared
        block = ctx.enter_context(nc.Block())

        @block.sync
        def _(sp):
            sp.wait_ge(s["x2_ready"], NB)
            sp.dma_start(a["rows"].rearrange("(b p) m -> p b m", p=P)[:, NB - TB:NB, 0:M],
                         x2[:, NB - TB:NB, :]).then_inc(s["x2_out"], 16)
            sp.wait_ge(s["r_score"], 1)
            sp.dma_start(a["rows"].rearrange("(b p) m -> p b m", p=P)[:, :, M:ROW],
                         score_rows[:]).then_inc(s["score_out"], 16)
            sp.wait_ge(s["h2_out"], 16 * B)
            sp.wait_ge(s["x2_out"], 16 * B)

        @block.gpsimd
        def _(pool):
            nc.gpsimd.memset(neg_half[:], -0.5).then_inc(s["r_const"], 1)
            pool.wait_ge(s["r_const"], 1)
            pool.wait_ge(s["r_aggr"], 1)
            nc.gpsimd.tensor_scalar(rstd[:], mean_var[:, :, 1], EPS, None, ALU.add)\
                .then_inc(s["r_eps"], 1)
            pool.wait_ge(s["r_eps"], 1)
            nc.gpsimd.tensor_tensor(rstd[:], rstd[:], neg_half[:], ALU.pow)\
                .then_inc(s["r_rstd"], 1)

        @block.vector
        def _(dve):
            step = [0]

            def chained(ins):
                step[0] += 1
                ins.then_inc(s["r_step"], 1)
                dve.wait_ge(s["r_step"], step[0])

            def copy_half(g):
                dve.wait_ge(s["r_tr"], 2 * g + 2)
                if g >= 2:
                    dve.wait_ge(s["r_logitsT"], g - 1)
                nc.vector.tensor_copy(xT[:, g % 2, 1, :], x_ps[g % 2][1][:])\
                    .then_inc(s["r_copy1"], 1)

            for tb in range(TB):
                last = nc.vector.bn_stats(stats[:, tb, :], h2[:, tb, :])
            chained(last)
            for tb in range(TB):
                last = nc.vector.bn_aggr(mean_var[:, tb, :], stats[:, tb, :])
            last.then_inc(s["r_aggr"], 1)
            for g in range(2):
                copy_half(g)
            dve.wait_ge(s["r_rstd"], 1)
            for tb in range(TB):
                nc.vector.tensor_scalar(x2[:, NB - TB + tb, :], h2[:, tb, :], mean_var[:, tb, 0:1],
                                        rstd[:, tb:tb + 1], ALU.subtract, ALU.mult)\
                    .then_inc(s["x2_ready"], 1)
            for g in range(2, NG):
                copy_half(g)
            dve.wait_ge(s["r_logits_done"], NG)
            chained(nc.vector.tensor_reduce(top[:], l_ps[:], AX.X, ALU.max))
            nc.vector.tensor_tensor(logit[:], l_ps[:], top[:].unsqueeze(2).to_broadcast([P, NB, E]),
                                    ALU.subtract).then_inc(s["r_exp"], 1)
            dve.wait_ge(s["r_exp"], 2)
            chained(nc.vector.tensor_reduce(total[:], logit[:], AX.X, ALU.add))
            chained(nc.vector.reciprocal(total[:], total[:]))
            nc.vector.tensor_tensor(score_rows[:], logit[:],
                                    total[:].unsqueeze(2).to_broadcast([P, NB, E]), ALU.mult)\
                .then_inc(s["r_score"], 1)
            nc.vector.tensor_tensor(score[:].rearrange("p e b -> p b e"), logit[:],
                                    total[:].unsqueeze(2).to_broadcast([P, NB, E]), ALU.mult)\
                .then_inc(s["r_score"], 1)

        @block.scalar
        def _(act):
            for g in range(NG + 1):
                if g < NG:
                    act.wait_ge(s["r_tr"], 2 * g + 1)
                    if g >= 2:
                        act.wait_ge(s["r_logitsT"], g - 1)
                    nc.scalar.activation(xT[:, g % 2, 0, :], x_ps[g % 2][0][:], ACT.Copy)\
                        .then_inc(s["r_copy0"], 1)
                if g >= 1:
                    u = g - 1
                    act.wait_ge(s["r_logitsT"], u + 1)
                    if u >= 2:
                        act.wait_ge(s["r_logits_done"], u - 1)
                    nc.scalar.activation(lT[:, u % 2, :], lT_ps[u % 2][:], ACT.Copy)\
                        .then_inc(s["r_lT"], 1)
            act.wait_ge(s["r_exp"], 1)
            nc.scalar.activation(logit[:], logit[:], ACT.Exp).then_inc(s["r_exp"], 1)

        @block.tensor
        def _(pe):
            pe.wait_ge(s["wr_in"], 16)
            for g in range(NG + 2):
                if g < NG:
                    pe.wait_ge(s["x2_ready"], TB * (g + 1))
                    for kt in range(KT):
                        if g >= 2:
                            pe.wait_ge(s[f"r_copy{kt}"], g - 1)
                        for tb in range(TB):
                            last = nc.tensor.transpose(x_ps[g % 2][kt][:, tb * P:(tb + 1) * P],
                                                       x2[:, TB * g + tb, kt * P:(kt + 1) * P],
                                                       ident[:])
                        last.then_inc(s["r_tr"], 1)
                if 1 <= g <= NG:
                    u = g - 1
                    if u >= 2:
                        pe.wait_ge(s["r_lT"], u - 1)
                    for kt in range(KT):
                        pe.wait_ge(s[f"r_copy{kt}"], u + 1)
                        last = nc.tensor.matmul(lT_ps[u % 2][:], wr[:, kt, :], xT[:, u % 2, kt, :],
                                                start=kt == 0, stop=kt == KT - 1)
                    last.then_inc(s["r_logitsT"], 1)
                if g >= 2:
                    u = g - 2
                    pe.wait_ge(s["r_lT"], u + 1)
                    for tb in range(TB):
                        last = nc.tensor.transpose(l_ps[:, TB * u + tb, :],
                                                   lT[:, u % 2, tb * P:(tb + 1) * P],
                                                   ident[0:E, 0:E])
                    last.then_inc(s["r_logits_done"], 1)


def build_experts(nc, a, ident, score, shared):
    ctx = ExitStack()
    with ctx:
        def sb(name, shape, dt=F32):
            return ctx.enter_context(nc.sbuf_tensor(name, shape, dt))

        def ps(name, shape=(P, 512)):
            return ctx.enter_context(nc.psum_tensor(name, list(shape), F32))

        groups_f, groups = sb("groups_f", [P, 2, P]), sb("groups", [P, 2, P], BF16)
        EH = 2
        scoreT = sb("scoreT", [P, EH, P])
        least = sb("least", [P, EH], I32)
        step_bits = sb("step_bits", [P, 3, EH], I32)
        step_f = sb("step_f", [P, EH])
        cand = sb("cand", [P, 3, EH], I32)
        hits = sb("hits", [P, 3, EH, P], BF16)
        count_bf = sb("count_bf", [P, 3, EH], BF16)
        enough = sb("enough", [P, 3, EH])
        steps = sb("steps", [P, EH])
        steps_i = sb("steps_i", [P, EH], I32)
        above, equal = sb("above", [P, EH, P]), sb("equal", [P, EH, P])
        chosen = sb("chosen", [P, EH, P])
        need = sb("need", [P, EH])
        base = sb("base", [P, EH])
        rank = sb("rank", [P, EH, P])
        all_ones = sb("all_ones", [P, P])
        place = sb("place", [P, E, NB], I32)
        place_a, place_b = sb("place_a", [P, E, NB], I32), sb("place_b", [P, E, NB], I32)
        at_a, at_b = sb("at_a", [P, E, NB], BF16), sb("at_b", [P, E, NB], BF16)
        iota_i = sb("iota_i", [P, LIST_A], I32)
        iota32 = sb("iota32", [P, LIST_A], BF16)
        blk_i = sb("blk_i", [P, NB], I32)
        blk_no = sb("blk_no", [P, NB], BF16)
        tok_i = sb("tok_i", [P, 1], I32)
        tok_no = sb("tok_no", [P, 1])
        hot_a = sb("hot_a", [P, NB, LIST_A], BF16)
        hot_b = sb("hot_b", [P, NB, 3, LIST_A], BF16)
        list_tok = sb("list_tok", [LIST_A, LIST_A])
        list_f = sb("list_f", [LIST_A, LIST_A])
        tokens = [sb(f"tokens{i}", [P, CH], I32) for i in range(2)]
        raw1, raw2 = sb("raw1", [P, KT, DI]), sb("raw2", [P, DT, M])
        w1 = [[sb(f"w1_{i}{p}", [P, KT, DI], F32R) for p in ("hi", "lo")] for i in range(2)]
        w2 = [[sb(f"w2_{i}{p}", [P, DT, M], F32R) for p in ("hi", "lo")] for i in range(2)]
        b1_rows = sb("b1_rows", [E * DT, P])
        b1 = sb("b1", [P, E * DT])
        b1_e = [sb(f"b1_e{i}", [P, DT]) for i in range(2)]
        b2 = sb("b2", [P, E, M])
        got = [sb(f"got{i}", [P, CH, ROW]) for i in range(2)]
        gate = [sb(f"gate{i}", [P, CH]) for i in range(2)]
        xT = [[sb(f"e_xT{i}{p}", [P, KT, TOPK], F32R) for p in ("hi", "lo")] for i in range(2)]
        hid = sb("hid", [P, 2, HALF])
        hT = [sb(f"hT_{p}", [P, 4, HALF], F32R) for p in ("hi", "lo")]
        y = [sb(f"y{i}", [P, TB, M]) for i in range(2)]

        up_ps = [ps("up0"), ps("up1")]
        y_ps = [[ps("y00"), ps("y01")], [ps("y10"), ps("y11")]]
        x_ps, l_ps = ps("x_ps"), ps("l_ps")

        names = """c_in b2_in c_const c_step counted totalled marked ranked turned b1_tr b1_ready
            raw_in w_hi2 w_lo2 up_done down_done h_hi h_lo e_xt_tr e_xt_hi e_xt_lo hot_ready listed
            tok_ready rows_in0 rows_in1 gate_ready y_b2 y_gated added0 added1 l_chain e_apart""".split()
        s = {n: ctx.enter_context(nc.semaphore(n)) for n in names} | shared
        block = ctx.enter_context(nc.Block())

        def after(eng, name, count):
            if isinstance(count, int) and count <= 0:
                return
            eng.wait_ge(s[name], count)

        def alone(eng):
            eng.sem_inc(s["e_apart"], 1)

        STEPS = 2 * DT
        RING = 4
        ITERATIONS = 15
        LAG = 2

        def experts(eng, body):
            for i in range(2):
                body(i, i, True)
            with eng.Fori(1, E // 2 - 1) as j:
                for i in range(2):
                    body(j * 2 + i, i, True)
            for i in range(2):
                body(E - 2 + i, i, i == 0)

        def wide(x):
            return x.unsqueeze(2).to_broadcast([P, E, NB])

        @block.sync
        def _(sp):
            sp.dma_start(groups_f[:], a["groups"][:, :, :]).then_inc(s["c_in"], 16)
            sp.dma_start(b1_rows[:], a["b1"].rearrange("e (t p) -> (e t) p", p=P))\
                .then_inc(s["c_in"], 16)
            sp.dma_start(b2[:], a["b2"].rearrange("(o e) m -> o e m", o=1).to_broadcast([P, E, M]))\
                .then_inc(s["b2_in"], 16)

            def load(e):
                after(sp, "w_lo2", 2 * e)
                sp.dma_start(raw1[:], a["w1"][e].rearrange("(t p) n -> p t n", p=P))\
                    .then_inc(s["raw_in"], 16)
                sp.dma_start(raw2[:], a["w2"][e].rearrange("(t p) m -> p t m", p=P))\
                    .then_inc(s["raw_in"], 16)
            load(0)
            experts(sp, lambda e, i, more: load(e + 1) if more else None)
            for half in range(2):
                sp.wait_ge(s[f"added{half}"], 16 * TB * E)

        @block.gpsimd
        def _(pool):
            nc.gpsimd.iota(iota_i[:], [[1, LIST_A]], base=0, channel_multiplier=0)\
                .then_inc(s["c_const"], 1)
            nc.gpsimd.iota(blk_i[:], [[1, NB]], base=0, channel_multiplier=0)\
                .then_inc(s["c_const"], 1)
            nc.gpsimd.iota(tok_i[:], [[1, 1]], base=0, channel_multiplier=1)\
                .then_inc(s["c_const"], 1)
            nc.gpsimd.memset(all_ones[:], 1.0).then_inc(s["c_const"], 1)
            nc.gpsimd.memset(least[:], 0).then_inc(s["c_const"], 1)
            nc.gpsimd.memset(step_f[:], float(1 << 28)).then_inc(s["c_const"], 1)
            for k in range(3):
                nc.gpsimd.memset(step_bits[:, k, :], (k + 1) << 28).then_inc(s["c_const"], 1)

            def gather(e, i):
                after(pool, "tok_ready", e + 1)
                after(pool, "e_xt_tr", 4 * (e - 1))
                after(pool, "gate_ready", e - 1)
                alone(pool)
                for c in range(CH):
                    pool.indirect_dma_start(got[i][:, c, :], None, a["rows"][:, :],
                                            bass.IndirectOffsetOnAxis(tokens[i][:, c:c + 1], 0))\
                        .then_inc(s[f"rows_in{c // TB}"], 16)

            def add(e, i, half):
                u = 2 * e + half
                after(pool, "gate_ready", e + 1)
                after(pool, "y_b2", 2 * u + 2)
                alone(pool)
                for c in range(TB):
                    nc.gpsimd.tensor_scalar(y[half][:, c, :], y[half][:, c, :],
                                            gate[i][:, TB * half + c:TB * half + c + 1], 1.0,
                                            ALU.mult, ALU.mult).then_inc(s["y_gated"], 1)
                if half == 0:
                    for k in range(2):
                        after(pool, f"added{k}", 16 * TB * e)
                for c in range(TB):
                    after(pool, "y_gated", TB * u + c + 1)
                    alone(pool)
                    pool.indirect_dma_start(a["out"][:, :],
                                            bass.IndirectOffsetOnAxis(
                                                tokens[i][:, TB * half + c:TB * half + c + 1], 0),
                                            y[half][:, c, :], None, compute_op=ALU.add)\
                        .then_inc(s[f"added{half}"], 16)

            pool.wait_ge(s["score_out"], 16)
            gather(0, 0)

            def body(e, i, more):
                if not (isinstance(e, int) and e == 0):
                    add(e - 1, 1 - i, 1)
                if more:
                    gather(e + 1, 1 - i)
                add(e, i, 0)
            experts(pool, body)
            add(E - 1, 1, 1)

        @block.vector
        def _(dve):
            step = [0]

            def chained(ins):
                step[0] += 1
                ins.then_inc(s["c_step"], 1)
                dve.wait_ge(s["c_step"], step[0])

            dve.wait_ge(s["c_const"], 9)
            nc.vector.tensor_copy(iota32[:], iota_i[:]).then_inc(s["l_chain"], 1)
            nc.vector.tensor_copy(blk_no[:], blk_i[:])
            chained(nc.vector.tensor_copy(tok_no[:], tok_i[:]))
            dve.wait_ge(s["turned"], 1)
            nc.vector.tensor_copy(scoreT[:].rearrange("p g t -> p (g t)"), x_ps[:, 0:EH * P])
            dve.wait_ge(s["c_in"], 32)
            chained(nc.vector.tensor_copy(groups[:], groups_f[:]))
            dve.wait_ge(s["b1_tr"], 1)
            nc.vector.tensor_copy(b1[:], l_ps[:, 0:E * DT]).then_inc(s["b1_ready"], 1)

            with dve.Fori(0, ITERATIONS) as r:
                dve.wait_ge(s["l_chain"], r * 4 + 1)
                nc.vector.tensor_tensor(cand[:], step_bits[:],
                                        least[:].unsqueeze(1).to_broadcast([P, 3, EH]),
                                        ALU.bitwise_or).then_inc(s["l_chain"], 1)
                dve.wait_ge(s["l_chain"], r * 4 + 2)
                with nc.allow_low_precision(reason="counts up to 128 are exact in bfloat16"):
                    for k in range(3):
                        for g in range(EH):
                            last = nc.vector.tensor_scalar(
                                hits[:, k, g, :], scoreT[:, g, :],
                                cand[:, k, g:g + 1].bitcast(F32), None, ALU.is_ge, ALU.add,
                                accum_out=count_bf[:, k, g:g + 1])
                last.then_inc(s["counted"], 1)
                nc.vector.tensor_scalar(step_bits[:], step_bits[:], 2, None,
                                        ALU.logical_shift_right)
                dve.wait_ge(s["totalled"], r + 1)
                for g in range(EH):
                    last = nc.vector.tensor_scalar(
                        enough[:, :, g], l_ps[:, 0:3 * EH].rearrange("p (k g) -> p k g", g=EH)[:, :, g],
                        float(TOPK), None, ALU.is_ge, ALU.add, accum_out=steps[:, g:g + 1])
                last.then_inc(s["l_chain"], 1)
                dve.wait_ge(s["l_chain"], r * 4 + 3)
                nc.vector.tensor_tensor(steps_i[:], steps[:], step_f[:], ALU.mult)\
                    .then_inc(s["l_chain"], 1)
                dve.wait_ge(s["l_chain"], r * 4 + 4)
                nc.vector.tensor_scalar(step_f[:], step_f[:], 0.25, None, ALU.mult)
                nc.vector.tensor_tensor(least[:], least[:], steps_i[:], ALU.bitwise_or)\
                    .then_inc(s["l_chain"], 1)
            dve.wait_ge(s["l_chain"], ITERATIONS * 4 + 1)

            def mark(out, op):
                with nc.allow_low_precision(reason="counts up to 128 are exact in bfloat16"):
                    for g in range(EH):
                        last = nc.vector.tensor_scalar(out[:, g, :], scoreT[:, g, :],
                                                       least[:, g:g + 1].bitcast(F32), None,
                                                       op, ALU.add, accum_out=count_bf[:, 0, g:g + 1])
                return last

            def ranks(marks, k):
                dve.wait_ge(s["ranked"], k)
                chained(nc.vector.tensor_copy(base[:], l_ps[:, 0:EH]))
                for g in range(EH):
                    last = nc.vector.tensor_tensor_scan(rank[:, g, :], all_ones[:], marks[:, g, :],
                                                        base[:, g:g + 1], ALU.mult, ALU.add)
                chained(last)

            mark(above, ALU.is_gt).then_inc(s["counted"], 1)
            dve.wait_ge(s["totalled"], ITERATIONS + 1)
            chained(nc.vector.tensor_scalar(need[:], l_ps[:, 0:EH], -1.0, float(TOPK),
                                            ALU.mult, ALU.add))
            mark(equal, ALU.is_equal).then_inc(s["marked"], 1)
            ranks(equal, 1)
            for g in range(EH):
                last = nc.vector.scalar_tensor_tensor(chosen[:, g, :], rank[:, g, :],
                                                      need[:, g:g + 1], equal[:, g, :],
                                                      ALU.is_le, ALU.mult)
            chained(last)
            chained(nc.vector.tensor_tensor(chosen[:], chosen[:], above[:], ALU.add))
            with nc.allow_low_precision(reason="counts up to 128 are exact in bfloat16"):
                nc.vector.tensor_reduce(count_bf[:, 0, :], chosen[:], AX.X, ALU.add)\
                    .then_inc(s["marked"], 1)
            ranks(chosen, 2)
            nc.vector.scalar_tensor_tensor(rank[:], chosen[:], -4.0 * TOPK, rank[:],
                                           ALU.mult, ALU.add).then_inc(s["marked"], 1)
            dve.wait_ge(s["turned"], 2)
            chained(nc.vector.tensor_scalar(place[:].rearrange("p e b -> p (e b)"),
                                            x_ps[:, 0:E * NB], 4.0 * TOPK - 1.0, None, ALU.add))
            chained(nc.vector.tensor_scalar(place_a[:], place[:], 5, None, ALU.logical_shift_right))
            chained(nc.vector.tensor_scalar(place_b[:], place[:], LIST_A - 1, None, ALU.bitwise_and))
            nc.vector.tensor_copy(at_a[:], place_a[:])
            chained(nc.vector.tensor_copy(at_b[:], place_b[:]))

            chain0 = ITERATIONS * 4 + 1

            def one_hots(e):
                after(dve, "listed", e)
                wide_iota = iota32[:].unsqueeze(1).to_broadcast([P, NB, LIST_A])

                def spread(x):
                    return x[:, bass.ds(e, 1), :].rearrange("p o b -> p (o b)").unsqueeze(2)\
                        .to_broadcast([P, NB, LIST_A])
                nc.vector.tensor_tensor(hot_a[:], spread(at_a), wide_iota, ALU.is_equal)
                nc.vector.tensor_tensor(hot_b[:, :, 0, :], spread(at_b), wide_iota, ALU.is_equal)\
                    .then_inc(s["l_chain"], 1)
                dve.wait_ge(s["l_chain"], e * 3 + (chain0 + 1))
                nc.vector.tensor_scalar(hot_b[:, :, 1, :], hot_b[:, :, 0, :], tok_no[:, 0:1], None,
                                        ALU.mult)
                nc.vector.tensor_tensor(hot_b[:, :, 2, :], hot_b[:, :, 0, :],
                                        blk_no[:].unsqueeze(2).to_broadcast([P, NB, LIST_A]),
                                        ALU.mult).then_inc(s["hot_ready"], 1)

            def write_list(e, i):
                after(dve, "listed", e + 1)
                for k in range(2):
                    after(dve, f"added{k}", 16 * TB * (e - 1))
                nc.vector.tensor_copy(list_tok[:], l_ps[0:LIST_A, 0:LIST_A]).then_inc(s["l_chain"], 1)
                dve.wait_ge(s["l_chain"], e * 3 + (chain0 + 2))
                nc.vector.scalar_tensor_tensor(list_f[:], l_ps[0:LIST_A, LIST_A:2 * LIST_A], float(P),
                                               list_tok[:], ALU.mult, ALU.add)\
                    .then_inc(s["l_chain"], 1)
                dve.wait_ge(s["l_chain"], e * 3 + (chain0 + 3))
                for q in range(P // LIST_A):
                    last = nc.vector.tensor_copy(
                        tokens[i][q * LIST_A:(q + 1) * LIST_A, :],
                        list_f[:].rearrange("a (c q) -> a q c", q=P // LIST_A)[:, q, :])
                last.then_inc(s["tok_ready"], 1)

            def low(out, in_, hi, name):
                nc.vector.tensor_tensor(out, in_, hi.bitcast(F32), ALU.subtract)\
                    .then_inc(s[name], 1)

            def split_weights(e, i, which):
                raw, w = ((raw1, w1), (raw2, w2))[which]
                after(dve, "w_hi2", 2 * e + which + 1)
                low(w[i][1][:], raw[:], w[i][0][:], "w_lo2")

            def first_bias(e, i):
                after(dve, "b1_ready", e + 1)
                after(dve, "h_hi", STEPS * (e - 1))
                nc.vector.tensor_scalar(b1_e[i][:], b1[:, bass.ds(e * DT, DT)], 1.0, None, ALU.mult)\
                    .then_inc(s["b1_ready"], 1)

            def gates(e, i):
                for half in range(2):
                    after(dve, f"rows_in{half}", 16 * TB * (e + 1))
                after(dve, "y_gated", CH * (e - 1))
                nc.vector.tensor_scalar(gate[i][:],
                                        got[i][:, :, bass.ds(e + M, 1)].rearrange("p c o -> p (c o)"),
                                        1.0, None, ALU.mult).then_inc(s["gate_ready"], 1)

            def xt_low(e, i, f):
                g, kt = divmod(f, 2)
                after(dve, "e_xt_hi", 4 * e + f + 1)
                cols = slice(g * HALF, (g + 1) * HALF)
                low(xT[i][1][:, kt, cols], x_ps[:], xT[i][0][:, kt, cols], "e_xt_lo")

            def results(e, half):
                u = 2 * e + half
                after(dve, "down_done", DT * (u + 1))
                after(dve, f"added{half}", 16 * TB * e)
                for k in range(2):
                    nc.vector.tensor_tensor(
                        y[half][:, 2 * k:2 * k + 2, :],
                        y_ps[half][k][:].rearrange("p (c m) -> p c m", m=M),
                        b2[:, bass.ds(e, 1), :].to_broadcast([P, 2, M]), ALU.add)\
                        .then_inc(s["y_b2"], 1)

            dve.wait_ge(s["b2_in"], 16)
            one_hots(0)
            write_list(0, 0)
            first_bias(0, 0)
            split_weights(0, 0, 0)
            split_weights(0, 0, 1)
            for f in range(2):
                xt_low(0, 0, f)

            def body(e, i, more):
                for t in range(STEPS):
                    k = e * STEPS + t
                    if more and t >= 12:
                        xt_low(e + 1, 1 - i, t - 12)
                    if more and t == 15:
                        gates(e + 1, 1 - i)
                    if isinstance(e, int) and e == 0 and t in (3, 4):
                        xt_low(0, 0, t - 1)
                    if isinstance(e, int) and e == 0 and t == 4:
                        gates(0, 0)
                    after(dve, "h_hi", k + 1)
                    low(hT[1][:, t % RING, :], hid[:, t % 2, :],
                        hT[0][:, t % RING, :], "h_lo")
                    if t == LAG and not (isinstance(e, int) and e == 0):
                        results(e - 1, 1)
                    if t == DT + LAG:
                        results(e, 0)
                    if more:
                        if t == 0:
                            one_hots(e + 1)
                        if t == 5:
                            write_list(e + 1, 1 - i)
                            first_bias(e + 1, 1 - i)
                        if t in (6, 8):
                            split_weights(e + 1, 1 - i, (t - 6) // 2)
            experts(dve, body)
            results(E - 1, 1)

        @block.scalar
        def _(act):
            def hi_of(out, in_, name):
                nc.scalar.activation(out, in_, ACT.Copy).then_inc(s[name], 1)

            def split_weights(e, i, which):
                raw, w = ((raw1, w1), (raw2, w2))[which]
                after(act, "raw_in", 32 * (e + 1))
                after(act, "down_done", STEPS * (e - 1))
                hi_of(w[i][0][:], raw[:], "w_hi2")

            def xt_high(e, i, f):
                g, kt = divmod(f, 2)
                after(act, "e_xt_tr", 4 * e + f + 1)
                after(act, "up_done", STEPS * (e - 1))
                hi_of(xT[i][0][:, kt, g * HALF:(g + 1) * HALF], x_ps[:], "e_xt_hi")

            split_weights(0, 0, 0)
            split_weights(0, 0, 1)
            for f in range(2):
                xt_high(0, 0, f)

            def body(e, i, more):
                after(act, "b1_ready", e + 2)
                for t in range(STEPS):
                    k = e * STEPS + t
                    if more and t >= 12:
                        xt_high(e + 1, 1 - i, t - 12)
                    if isinstance(e, int) and e == 0 and t in (3, 4):
                        xt_high(0, 0, t - 1)
                    bias = b1_e[i][:, t % DT:t % DT + 1]
                    after(act, "up_done", k + 1)
                    after(act, "h_lo", k - 1)
                    nc.scalar.activation(hid[:, t % 2, :], up_ps[t % 2][:], ACT.Gelu, bias=bias)
                    after(act, "down_done", k - (RING - 1))
                    nc.scalar.activation(hT[0][:, t % RING, :], up_ps[t % 2][:], ACT.Gelu,
                                         bias=bias).then_inc(s["h_hi"], 1)
                    if more:
                        if t in (5, 7):
                            split_weights(e + 1, 1 - i, (t - 5) // 2)
            experts(act, body)

        @block.tensor
        def _(pe):
            PARTS = [(0, 0), (0, 1), (1, 0)]

            def turn_halves(out, in_):
                for g in range(EH):
                    last = nc.tensor.transpose(out[:, g * P:(g + 1) * P], in_[:, g, :], ident[:])
                last.then_inc(s["turned"], 1)

            def total(which, out):
                return nc.tensor.matmul(out, groups[:, which, :],
                                        count_bf[:].rearrange("p k g -> p (k g)")
                                        [:, 0:out.shape[1]], start=True, stop=True)

            turn_halves(x_ps, score[:].rearrange("p (g e) b -> p g (e b)", g=EH))
            pe.wait_ge(s["c_in"], 32)
            nc.tensor.transpose(l_ps[:, 0:E * DT], b1_rows[:], ident[0:E * DT, 0:E * DT])\
                .then_inc(s["b1_tr"], 1)
            pe.wait_ge(s["b1_ready"], 1)
            with pe.Fori(0, ITERATIONS) as r:
                pe.wait_ge(s["counted"], r + 1)
                total(0, l_ps[:, 0:3 * EH]).then_inc(s["totalled"], 1)
            pe.wait_ge(s["counted"], ITERATIONS + 1)
            total(0, l_ps[:, 0:EH]).then_inc(s["totalled"], 1)
            for k in range(2):
                pe.wait_ge(s["marked"], k + 1)
                total(1, l_ps[:, 0:EH]).then_inc(s["ranked"], 1)
            pe.wait_ge(s["marked"], 3)
            turn_halves(x_ps, rank)

            def write_list(e):
                after(pe, "hot_ready", e + 1)
                after(pe, "tok_ready", e)
                for t in range(NB):
                    last = nc.tensor.matmul(l_ps[0:LIST_A, 0:2 * LIST_A], hot_a[:, t, :],
                                            hot_b[:, t, 1:3, :].rearrange("p k b -> p (k b)"),
                                            start=t == 0, stop=t == NB - 1)
                last.then_inc(s["listed"], 1)

            def turn(e, i, f):
                g, kt = divmod(f, 2)
                after(pe, f"rows_in{g}", 16 * TB * (e + 1))
                after(pe, "e_xt_lo", 4 * e + f)
                for c in range(TB):
                    last = nc.tensor.transpose(x_ps[:, c * P:(c + 1) * P],
                                               got[i][:, TB * g + c, kt * P:(kt + 1) * P], ident[:])
                last.then_inc(s["e_xt_tr"], 1)

            def up(e, i, t):
                k = e * STEPS + t
                half, dt = divmod(t, DT)
                after(pe, "h_hi", k - 1)
                todo = [(w1[i][x][:, kt, dt * P:(dt + 1) * P],
                         xT[i][z][:, kt, half * HALF:(half + 1) * HALF])
                        for kt in range(KT) for x, z in PARTS]
                for c, (l, r) in enumerate(todo):
                    last = nc.tensor.matmul(up_ps[t % 2][:], l, r, start=c == 0,
                                            stop=c == len(todo) - 1)
                last.then_inc(s["up_done"], 1)

            def down(e, i, t):
                k = e * STEPS + t
                half, dt = divmod(t, DT)
                if dt == 0:
                    after(pe, "y_b2", e * 4 + 2 * half - 2)
                after(pe, "h_lo", k + 1)
                for c in range(TB):
                    for n, (x, z) in enumerate(PARTS):
                        last = nc.tensor.matmul(
                            y_ps[half][c // 2][:, (c % 2) * M:(c % 2 + 1) * M],
                            hT[x][:, t % RING, c * P:(c + 1) * P], w2[i][z][:, dt, :],
                            start=dt == 0 and c % 2 == 0 and n == 0,
                            stop=dt == DT - 1 and c % 2 == 1 and n == 2)
                last.then_inc(s["down_done"], 1)

            write_list(0)
            for f in range(2):
                turn(0, 0, f)

            def body(e, i, more):
                for t in range(STEPS):
                    if t == 0:
                        after(pe, "e_xt_lo", 4 * e + 2)
                        after(pe, "w_lo2", 2 * e + 2)
                    if t == DT:
                        after(pe, "e_xt_lo", 4 * e + 4)
                    up(e, i, t)
                    if t >= LAG:
                        down(e, i, t - LAG)
                    elif not (isinstance(e, int) and e == 0):
                        down(e - 1, 1 - i, STEPS + t - LAG)
                    if more and t == 2:
                        write_list(e + 1)
                    if more and 11 <= t < 15:
                        turn(e + 1, 1 - i, t - 11)
                    if isinstance(e, int) and e == 0 and t in (2, 3):
                        turn(0, 0, t)
            experts(pe, body)
            for t in range(LAG):
                down(E - 1, 1, STEPS + t - LAG)


def build(nc, a):
    ctx = ExitStack()
    with ctx:
        def sb(name, shape):
            return ctx.enter_context(nc.sbuf_tensor(name, shape, F32))

        score, score_rows = sb("score", [P, E, NB]), sb("score_rows", [P, NB, E])
        ident = sb("ident", [P, P])
        shared = {n: ctx.enter_context(nc.semaphore(n))
                  for n in "wr_in x2_ready h2_out x2_out score_out".split()}
        with (nc.sbuf_tensor("x2", [P, NB, M], F32) as x2, nc.sbuf_tensor("h2", [P, TB, M], F32) as h2,
              nc.sbuf_tensor("wr", [P, KT, E], F32) as wr):
            build_attention(nc, a, ident, h2, x2, wr, shared)
            build_router(nc, a, ident, h2, x2, wr, score, score_rows, shared)
        build_experts(nc, a, ident, score, shared)


def kernel(x, L0_tok_weight, L0_attn_w_aq, L0_attn_w_ak, L0_attn_w_av, L0_attn_w_ao,
           L0_ffn_Wr, L0_ffn_W1, L0_ffn_b1, L0_ffn_W2, L0_ffn_b2):
    import numpy as np
    import concourse.bacc as bacc
    from concourse.bass_utils import run_bass_kernel_spmd

    half = D // 2
    freqs = np.power(np.float32(10000.0), -np.arange(half, dtype=np.float32) / np.float32(half))
    angles = np.arange(T, dtype=np.float32)[None, :] * freqs[:, None].astype(np.float32)
    cos, sin = np.cos(angles), np.sin(angles)
    rope = np.stack([np.concatenate([cos, cos]), np.concatenate([-sin, sin])], 1)
    i = np.arange(P)
    later = i[None, :] > i[:, None]
    same = i[None, :] // NB == i[:, None] // NB

    arrays = {
        "ids": np.ascontiguousarray(x.reshape(B, TB, P).transpose(0, 2, 1)),
        "emb": L0_tok_weight,
        "wq": L0_attn_w_aq.reshape(M, H * D), "wk": L0_attn_w_ak.reshape(M, H * D),
        "wv": L0_attn_w_av.reshape(M, H * D), "wo": L0_attn_w_ao,
        "wr": L0_ffn_Wr, "w1": L0_ffn_W1, "b1": L0_ffn_b1, "w2": L0_ffn_W2, "b2": L0_ffn_b2,
        "rope": rope.astype(np.float32), "ident": np.eye(P, dtype=np.float32),
        "mask": np.where(later, np.float32(1e30), np.float32(0)),
        "groups": np.stack([same, same & later], 1).astype(np.float32),
    }
    arrays = {k: np.ascontiguousarray(v) for k, v in arrays.items()}
    nc = bacc.Bacc("TRN2", target_bir_lowering=False, num_devices=1)
    a = {k: nc.dram_tensor(f"in_{k}", v.shape, mybir.dt.from_np(v.dtype), kind="ExternalInput").ap()
         for k, v in arrays.items()}
    a["out"] = nc.dram_tensor("out_0", (N, M), F32, kind="ExternalOutput").ap()
    a["rows"] = nc.dram_tensor("routed_rows", (N, ROW), F32, kind="Internal").ap()
    build(nc, a)
    r = run_bass_kernel_spmd(nc, [{f"in_{k}": v for k, v in arrays.items()}], core_ids=[0])
    return r.results[0]["out_0"].reshape(B, T, M)
```
